# Optimizing a Trainium2 kernel written in Bass

```python
import numpy as np
import jax
import jax.numpy as jnp

def _softmax(x, axis=-1):
    return jax.nn.softmax(x, axis=axis)

def _gelu(x):
    return jax.nn.gelu(x, approximate=True)

def _silu(x):
    return jax.nn.silu(x)

def _sigmoid(x):
    return jax.nn.sigmoid(x)

def _layernorm(x, axis=-1, eps=1e-05):
    m = jnp.mean(x, axis=axis, keepdims=True)
    v = jnp.var(x, axis=axis, keepdims=True)
    return (x - m) / jnp.sqrt(v + eps)

def _scatter_add(tgt, idx, src, axis=0):
    return tgt.at[idx].add(src)

def _segment_sum(src, seg, n):
    return jax.ops.segment_sum(src, seg, n)
kernel_name = 'mk_adj_preln_d2_adj_r2_a3d46f'

def setup_inputs(seed: int=0):
    np.random.seed(seed)
    _w = jnp.asarray

    def _rec_inputs():
        import jax
        import jax.numpy as jnp
        _gk = jax.random.key(seed)
        x = -0.0003929 + 0.9999 * jax.random.normal(jax.random.fold_in(_gk, 1), (64, 128, 256), jnp.float32)
        _w = (1.0 + jnp.arange(128, dtype=jnp.float32)) ** (-0.5)
        _w = _w / _w.mean()
        _pij = jnp.clip(0.03125 * _w[:, None] * _w[None, :], 0.0, 1.0)
        _a = jax.random.uniform(jax.random.fold_in(_gk, 2), (64, 128, 128)) < _pij
        _a = jnp.logical_or(_a, jnp.swapaxes(_a, -1, -2))
        _a = jnp.logical_or(_a, jnp.eye(128, dtype=bool))
        _af = _a.astype(jnp.float32)
        _af = _af * jax.random.uniform(jax.random.fold_in(_gk, 3), (64, 128, 128), jnp.float32, 0.05, 1)
        adj = _af
        _nm = jnp.ones((64, 128), dtype=bool)
        nodemask = jnp.where(_nm, 1.0, 0.0).astype(jnp.float32)
        return (x, adj, nodemask)
    x, adj, nodemask = _rec_inputs()

    def _L0_gnn_setup():
        import jax, jax.numpy as jnp
        import numpy as np
        B, N, F_IN, F_HID, F_OUT = (32, 512, 256, 256, 256)

        def _gcn_layer(x, adj, W, b):
            support = jnp.einsum('bnf,fh->bnh', x, W)
            return jnp.einsum('bnm,bmh->bnh', adj, support) + b
        key = jax.random.key(seed)
        ks = jax.random.split(key, 8)

        def xavier(k, fan_in, fan_out):
            bound = float(np.sqrt(6.0 / (fan_in + fan_out)))
            return jax.random.uniform(k, (fan_in, fan_out), jnp.float32, -bound, bound)
        return {'batch_graph': jax.random.normal(ks[0], (B, N, F_IN), jnp.float32), 'adj': jax.random.uniform(ks[1], (B, N, N), jnp.float32), 'W1': xavier(ks[2], F_IN, F_HID), 'b1': jnp.zeros((F_HID,), jnp.float32), 'W2': xavier(ks[3], F_HID, F_HID), 'b2': jnp.zeros((F_HID,), jnp.float32), 'W3': xavier(ks[4], F_HID, F_OUT), 'b3': jnp.zeros((F_OUT,), jnp.float32)}
    _L0_gnn_all = _L0_gnn_setup()
    _L0_gnn_in = {k: v for k, v in _L0_gnn_all.items() if k in ('W1', 'b1', 'W2', 'b2', 'W3', 'b3')}
    del _L0_gnn_all

    def _L1_gnn_setup():
        import jax, jax.numpy as jnp
        import numpy as np
        B, N, IN_DIM, ATT_DIM = (2, 4096, 256, 256)
        key = jax.random.key(seed)
        k1, k2, k3, k4 = jax.random.split(key, 4)
        X = jax.random.normal(k1, (B, N, IN_DIM), dtype=jnp.float32)
        adj = jax.random.uniform(k2, (B, N, N), dtype=jnp.float32)
        mask = jnp.ones((B, N), dtype=jnp.float32)
        Wqk = jax.random.normal(k3, (IN_DIM, 2 * ATT_DIM), dtype=jnp.float32) / np.sqrt(IN_DIM)
        Wv = jax.random.normal(k4, (IN_DIM, IN_DIM), dtype=jnp.float32) / np.sqrt(IN_DIM)
        return {'X': X, 'adj': adj, 'mask': mask, 'Wqk': Wqk, 'Wv': Wv}
    _L1_gnn_all = _L1_gnn_setup()
    _L1_gnn_in = {k: v for k, v in _L1_gnn_all.items() if k in ('Wqk', 'Wv')}
    del _L1_gnn_all
    return {'x': x, 'adj': adj, 'nodemask': nodemask, 'L0_gnn_W1': _L0_gnn_in['W1'], 'L0_gnn_b1': _L0_gnn_in['b1'], 'L0_gnn_W2': _L0_gnn_in['W2'], 'L0_gnn_b2': _L0_gnn_in['b2'], 'L0_gnn_W3': _L0_gnn_in['W3'], 'L0_gnn_b3': _L0_gnn_in['b3'], 'L1_gnn_Wqk': _L1_gnn_in['Wqk'], 'L1_gnn_Wv': _L1_gnn_in['Wv']}

def reference(x, adj, nodemask, L0_gnn_W1, L0_gnn_b1, L0_gnn_W2, L0_gnn_b2, L0_gnn_W3, L0_gnn_b3, L1_gnn_Wqk, L1_gnn_Wv):
    import jax
    import jax.numpy as jnp

    def _L0_gnn_ref(batch_graph, adj, W1, b1, W2, b2, W3, b3):
        import jax, jax.numpy as jnp
        import numpy as np
        B, N, F_IN, F_HID, F_OUT = (32, 512, 256, 256, 256)

        def _gcn_layer(x, adj, W, b):
            support = jnp.einsum('bnf,fh->bnh', x, W)
            return jnp.einsum('bnm,bmh->bnh', adj, support) + b
        x = jax.nn.relu(_gcn_layer(batch_graph, adj, W1, b1))
        x = jax.nn.relu(_gcn_layer(x, adj, W2, b2))
        out = _gcn_layer(x, adj, W3, b3)
        return out

    def _L1_gnn_ref(X, adj, mask, Wqk, Wv):
        import jax, jax.numpy as jnp
        import numpy as np
        B, N, IN_DIM, ATT_DIM = (2, 4096, 256, 256)
        qk = X @ Wqk
        q, k = jnp.split(qk, 2, axis=-1)
        v = X @ Wv
        att_dim = q.shape[-1]
        inv_scale = 1.0 / jnp.sqrt(jnp.float32(att_dim))
        k_m = k * mask[:, :, None]
        agg = jnp.einsum('bij,bjd->bid', adj, k_m)
        w = inv_scale * mask * jnp.einsum('bid,bid->bi', q, agg)
        L = jax.nn.softmax(w, axis=1)[:, :, None] * v
        return L
    h = jnp.maximum(_layernorm(x, axis=-1), 0.0)
    x = x + _L0_gnn_ref(h, adj, L0_gnn_W1, L0_gnn_b1, L0_gnn_W2, L0_gnn_b2, L0_gnn_W3, L0_gnn_b3)
    h = jnp.maximum(_layernorm(x, axis=-1), 0.0)
    x = x + _L1_gnn_ref(h, adj, nodemask, L1_gnn_Wqk, L1_gnn_Wv)
    return x

_drawn_inputs = setup_inputs


def setup_inputs(seed=0):
    import zlib

    import numpy as np

    out = dict(_drawn_inputs(seed))
    spreads = {'L0_gnn_b1': (0.0, 0.1), 'L0_gnn_b2': (0.0, 0.8), 'L0_gnn_b3': (0.0, 2.0)}
    factors = {'L1_gnn_Wqk': 41.095, 'L1_gnn_Wv': 40.999}
    for name, (base, spread) in spreads.items():
        noise = np.random.default_rng([zlib.crc32(name.encode()), seed]).standard_normal(out[name].shape)
        drawn = base * np.exp(spread * noise) if base else spread * noise
        out[name] = jnp.asarray(drawn.astype(out[name].dtype))
    for name, factor in factors.items():
        out[name] = (out[name] * factor).astype(out[name].dtype)
    return out
```

```python
from contextlib import ExitStack

import concourse.bass as bass
from concourse import mybir

F32 = mybir.dt.float32
F32R = mybir.dt.float32r
ALU = mybir.AluOpType
ACT = mybir.ActivationFunctionType

P = 128
GB = 2
RING = 4
EPS = 1e-5

D_LN1 = D_ADJT = 0
D_ZT = D_O1 = D_S2 = D_MASK = 1
D_O2 = D_S3 = D_X1 = 2
D_LN2 = D_H2T = D_TT = 3
D_SC = D_SOFTMAX = D_V = 4
LAST_DELAY = 4
AHEAD = 2


class Pair:

    def __init__(self, i, c):
        self.i, self.c = i, c

    def back(self, n):
        return Pair(self.i, self.c - n)

    def exists(self, pairs):
        return not isinstance(self.i, int) or 0 <= self.c < pairs

    def number(self):
        return self.i * RING + self.c

    def done(self):
        return self.i * RING + (self.c + 1)

    def landed(self):
        return self.i * 16 + 16 * (self.c // RING + 1)


def gnn_kernel(nc, x, adj, mask, W1, b1, W2, b2, W3, b3, Wqk, Wv, out):
    B, N, F = x.shape
    assert N == P and F == 2 * P
    C = F // P
    PAIRS = B // GB
    SCALE = float(F) ** -0.5

    FIRST = D_X1 + RING
    LOOPS = (PAIRS - FIRST - AHEAD) // RING
    TAIL = FIRST + LOOPS * RING
    ROUNDS = PAIRS + LAST_DELAY

    with ExitStack() as ctx:
        def sb(name, shape, dt=F32):
            return ctx.enter_context(nc.sbuf_tensor(name, shape, dt))

        def ring(name, n, shape, dt=F32):
            return [sb(f"{name}{k}", shape, dt) for k in range(n)]

        def bank(name):
            return ctx.enter_context(nc.psum_tensor(name, [P, 512], F32))

        def sem(name):
            return ctx.enter_context(nc.semaphore(name))

        ident = sb("ident", [P, P])
        minus_half = sb("minus_half", [P, GB])
        b1_col = sb("b1_col", [P, C])
        b2_col = sb("b2_col", [P, C])
        b3_all = sb("b3_all", [P, GB, F])
        raw = {k: sb(f"{k}_raw", [P, C, F]) for k in ("w1", "w2", "w3", "wv")}
        qk_raw = sb("qk_raw", [P, C, 2 * F])
        qT = sb("qT", [P, C, F])
        kT = sb("kT", [P, C, F])
        hi = {k: sb(f"{k}_hi", [P, C, F], F32R) for k in ("w1", "w2", "w3", "wv", "m")}
        lo = {k: sb(f"{k}_lo", [P, C, F], F32R) for k in ("w1", "w2", "w3", "wv", "m")}

        x_in = ring("x_in", RING, [P, GB, F])
        adj_in = ring("adj_in", RING, [P, GB, P])
        mask_all = ring("mask_all", RING, [P, GB, P])
        mask_row = ring("mask_row", RING, [GB, P])
        adj_masked = ring("adj_masked", RING, [P, GB, P])
        x_b3 = ring("x_b3", RING, [P, GB, F])
        stats1 = ring("stats1", 2, [P, GB, 6])
        stats2 = ring("stats2", 2, [P, GB, 6])
        mv1 = ring("mv1", 2, [P, GB, 2])
        mv2 = ring("mv2", 2, [P, GB, 2])
        ve1 = ring("ve1", 2, [P, GB])
        ve2 = ring("ve2", 2, [P, GB])
        rstd1 = ring("rstd1", 2, [P, GB])
        rstd2 = ring("rstd2", 2, [P, GB])
        xn = ring("xn", 2, [P, GB, F])
        h_full = ring("h_full", 2, [P, GB, F])
        h_hi = ring("h_hi", 2, [P, GB, F], F32R)
        h_lo = ring("h_lo", 2, [P, GB, F], F32R)
        aT_hi = ring("aT_hi", RING, [P, GB, P], F32R)
        aT_lo = ring("aT_lo", RING, [P, GB, P], F32R)
        zT_hi = ring("zT_hi", 2, [P, C, GB, P], F32R)
        zT_lo = ring("zT_lo", 2, [P, C, GB, P], F32R)
        o1_full = ring("o1_full", 2, [P, C, GB, P])
        o1_hi = ring("o1_hi", 2, [P, C, GB, P], F32R)
        o1_lo = ring("o1_lo", 2, [P, C, GB, P], F32R)
        s2_hi = ring("s2_hi", 2, [P, GB, F], F32R)
        s2_lo = ring("s2_lo", 2, [P, GB, F], F32R)
        o2_full = ring("o2_full", 2, [P, C, GB, P])
        o2_hi = ring("o2_hi", 2, [P, C, GB, P], F32R)
        o2_lo = ring("o2_lo", 2, [P, C, GB, P], F32R)
        s3_hi = ring("s3_hi", 2, [P, GB, F], F32R)
        s3_lo = ring("s3_lo", 2, [P, GB, F], F32R)
        x1 = ring("x1", RING, [P, GB, F])
        x1n = ring("x1n", 2, [P, GB, F])
        h2T = ring("h2T", 2, [P, C, GB, 2, P], F32R)
        h2T_hi = [t[:, :, :, 0, :] for t in h2T]
        h2T_lo = [t[:, :, :, 1, :] for t in h2T]
        tT_hi = ring("tT_hi", 2, [P, C, GB, P], F32R)
        tT_lo = ring("tT_lo", 2, [P, C, GB, P], F32R)
        weighed = ring("weighed", 2, [P, 2, P])
        w_col = ring("w_col", 2, [P, GB])
        w_row = ring("w_row", 2, [GB, P])
        w_max = ring("w_max", 2, [GB, 1])
        w_negmax = ring("w_negmax", 2, [GB, 1])
        e_row = ring("e_row", 2, [GB, P])
        e_sum = ring("e_sum", 2, [GB, 1])
        e_inv = ring("e_inv", 2, [GB, 1])
        p_row = ring("p_row", 2, [GB, P])
        p_col = ring("p_col", 2, [P, GB])

        bank_zT_s3 = bank("bank_zT_s3")
        bank_o2_tT = bank("bank_o2_tT")
        bank_sc_s2 = bank("bank_sc_s2")
        bank_aT_x1 = bank("bank_aT_x1")
        bank_h2T = bank("bank_h2T")
        bank_o1 = bank("bank_o1")
        bank_v = bank("bank_v")
        bank_w = bank("bank_w")

        def chunk_first(bank):
            return bank[:, :].rearrange("p (c g n) -> p c g n", c=C, g=GB)

        def graph_first(bank):
            return bank[:, :].rearrange("p (g f) -> p g f", g=GB)

        ps_zT, ps_s3 = chunk_first(bank_zT_s3), graph_first(bank_zT_s3)
        ps_o2, ps_tT = chunk_first(bank_o2_tT), chunk_first(bank_o2_tT)
        ps_sc, ps_s2 = graph_first(bank_sc_s2), graph_first(bank_sc_s2)
        ps_aT, ps_x1 = bank_aT_x1[:, 0:GB * P].rearrange("p (g n) -> p g n", g=GB), graph_first(bank_aT_x1)
        ps_h2T, ps_o1, ps_v = chunk_first(bank_h2T), chunk_first(bank_o1), graph_first(bank_v)
        ps_wrow = bank_w[0:GB, 0:P]
        ps_pcol = bank_w[:, P:P + GB]
        ps_qT, ps_kT, ps_m = graph_first(bank_h2T), graph_first(bank_v), graph_first(bank_w)

        weight_loaded = {k: sem(f"{k}_loaded") for k in ("w1", "w2", "w3", "wv", "qk")}
        bias_loaded = sem("bias_loaded")
        ident_zeroed = sem("ident_zeroed")
        const_made = sem("const_made")
        waits_passed = sem("waits_passed")
        weight_hi_made = sem("weight_hi_made")
        weight_lo_made = sem("weight_lo_made")
        qkT_transposed = sem("qkT_transposed")
        qT_copied = sem("qT_copied")
        kT_copied = sem("kT_copied")
        m_multiplied = sem("m_multiplied")
        x_loaded = [sem(f"x_loaded{k}") for k in range(RING)]
        adj_loaded = [sem(f"adj_loaded{k}") for k in range(RING)]
        mask_loaded = [sem(f"mask_loaded{k}") for k in range(RING)]
        row_loaded = [sem(f"row_loaded{k}") for k in range(RING)]
        out_stored = [sem(f"out_stored{k}") for k in range(RING)]
        adj_masked_made = sem("adj_masked_made")
        x_b3_made = sem("x_b3_made")
        stats1_made = sem("stats1_made")
        stats2_made = sem("stats2_made")
        mv1_made = sem("mv1_made")
        mv2_made = sem("mv2_made")
        ve1_made = sem("ve1_made")
        ve2_made = sem("ve2_made")
        rstd1_made = sem("rstd1_made")
        rstd2_made = sem("rstd2_made")
        xn_made = sem("xn_made")
        h_full_made = sem("h_full_made")
        h_hi_made = sem("h_hi_made")
        h_lo_made = sem("h_lo_made")
        aT_done = sem("aT_done")
        aT_hi_made = sem("aT_hi_made")
        aT_lo_made = sem("aT_lo_made")
        zT_done = sem("zT_done")
        zT_hi_made = sem("zT_hi_made")
        zT_lo_made = sem("zT_lo_made")
        o1_done = sem("o1_done")
        o1_full_made = sem("o1_full_made")
        o1_hi_made = sem("o1_hi_made")
        o1_lo_made = sem("o1_lo_made")
        s2_done = sem("s2_done")
        s2_hi_made = sem("s2_hi_made")
        s2_lo_made = sem("s2_lo_made")
        o2_done = sem("o2_done")
        o2_full_made = sem("o2_full_made")
        o2_hi_made = sem("o2_hi_made")
        o2_lo_made = sem("o2_lo_made")
        s3_done = sem("s3_done")
        s3_hi_made = sem("s3_hi_made")
        s3_lo_made = sem("s3_lo_made")
        x1_done = sem("x1_done")
        x1_made = sem("x1_made")
        x1n_made = sem("x1n_made")
        h2T_done = sem("h2T_done")
        h2T_hi_made = sem("h2T_hi_made")
        h2T_lo_made = sem("h2T_lo_made")
        tT_done = sem("tT_done")
        tT_hi_made = sem("tT_hi_made")
        tT_lo_made = sem("tT_lo_made")
        sc_done = sem("sc_done")
        w_col_made = sem("w_col_made")
        w_turned = sem("w_turned")
        w_row_made = sem("w_row_made")
        w_negmax_made = sem("w_negmax_made")
        e_made = sem("e_made")
        e_inv_made = sem("e_inv_made")
        p_row_made = sem("p_row_made")
        p_turned = sem("p_turned")
        p_col_made = sem("p_col_made")
        v_done = sem("v_done")
        out_made = sem("out_made")

        def standing_wait(eng, made, count):
            eng.wait_ge(made, count)
            eng.sem_inc(waits_passed, 1)

        def rounds(eng, one_round, prepare=lambda u: None):
            for u in range(FIRST):
                prepare(u)
                one_round(lambda delay: Pair(0, u - delay))
            with eng.Fori(0, LOOPS, 1) as i:
                for j in range(RING):
                    one_round(lambda delay: Pair(i, FIRST + j - delay))
            for u in range(TAIL, ROUNDS):
                one_round(lambda delay: Pair(0, u - delay))

        block = ctx.enter_context(nc.Block())

        @block.sync
        def _(sp):
            def load(p):
                if not p.exists(PAIRS):
                    return
                k, old, first = p.c % RING, p.back(RING), p.number() * GB
                again = old.exists(PAIRS)
                if again:
                    sp.wait_ge(xn_made, old.done())
                    sp.wait_ge(x_b3_made, old.done())
                sp.dma_start(x_in[k][:], x[bass.ds(first, GB)].rearrange("g n f -> n g f")).then_inc(x_loaded[k], 16)
                if again:
                    sp.wait_ge(aT_done, old.done())
                    sp.wait_ge(adj_masked_made, old.done())
                sp.dma_start(adj_in[k][:], adj[bass.ds(first, GB)].rearrange("g n m -> n g m")).then_inc(adj_loaded[k], 16)
                sp.dma_start(mask_all[k][:], mask[bass.ds(first, GB)].partition_broadcast(P)).then_inc(mask_loaded[k], 16)

            def load_row(p):
                if p.exists(PAIRS):
                    k, old = p.c % RING, p.back(RING)
                    if old.exists(PAIRS):
                        sp.wait_ge(w_row_made, old.done())
                    sp.dma_start(mask_row[k][:], mask[bass.ds(p.number() * GB, GB)]).then_inc(row_loaded[k], 16)

            def store(p):
                if p.exists(PAIRS):
                    k = p.c % RING
                    sp.wait_ge(out_made, p.done())
                    sp.dma_start(out[bass.ds(p.number() * GB, GB)].rearrange("g n f -> n g f"), x1[k][:]).then_inc(out_stored[k], 16)

            def load_weight(name, dst, src):
                sp.dma_start(dst[:], src.rearrange("(c f) h -> f c h", f=P)).then_inc(weight_loaded[name], 16)

            load(Pair(0, 0))
            load_weight("w1", raw["w1"], W1)
            load(Pair(0, 1))
            load_weight("w2", raw["w2"], W2)
            load_weight("qk", qk_raw, Wqk)
            load_weight("w3", raw["w3"], W3)
            load_weight("wv", raw["wv"], Wv)

            def one_round(at):
                load(at(-AHEAD))
                load_row(at(D_ZT))
                store(at(D_V))

            rounds(sp, one_round)
            for k in range(RING):
                sp.wait_ge(out_stored[k], 16 * (PAIRS // RING))

        @block.gpsimd
        def _(pool):
            pool.memset(ident[:], 0.0).then_inc(ident_zeroed, 1)
            pool.memset(minus_half[:], -0.5).then_inc(const_made, 1)
            pool.wait_ge(ident_zeroed, 1)
            pool.affine_select(out=ident[:], in_=ident[:], compare_op=ALU.not_equal, fill=1.0, base=0,
                               pattern=[[-1, P]], channel_multiplier=1).then_inc(const_made, 1)
            pool.wait_ge(const_made, 2)

            def variance_to_rstd(p, mv_made, mv, ve_made, ve, rstd_made, rstd, used):
                if p.exists(PAIRS):
                    k = p.c % 2
                    if p.back(2).exists(PAIRS):
                        pool.wait_ge(used, p.back(2).done())
                    standing_wait(pool, mv_made, p.done())
                    pool.tensor_scalar(ve[k][:], mv[k][:, :, 1], EPS, None, ALU.add).then_inc(ve_made, 1)
                    pool.wait_ge(ve_made, p.done())
                    pool.tensor_tensor(rstd[k][:], ve[k][:], minus_half[:], ALU.pow).then_inc(rstd_made, 1)

            def low_half(p, full_made, full, hi_made, high, low, lo_made):
                if p.exists(PAIRS):
                    k = p.c % 2
                    pool.wait_ge(full_made, p.done())
                    pool.wait_ge(hi_made, p.done())
                    pool.tensor_tensor(low[k][:], full[k][:], high[k][:].bitcast(F32), ALU.subtract).then_inc(lo_made, 1)

            def one_round(at):
                variance_to_rstd(at(D_LN2), mv2_made, mv2, ve2_made, ve2, rstd2_made, rstd2, x1n_made)
                variance_to_rstd(at(D_LN1), mv1_made, mv1, ve1_made, ve1, rstd1_made, rstd1, xn_made)
                p = at(D_MASK)
                if p.exists(PAIRS):
                    k = p.c % RING
                    pool.wait_ge(adj_loaded[k], p.landed())
                    pool.wait_ge(mask_loaded[k], p.landed())
                    if p.back(RING).exists(PAIRS):
                        pool.wait_ge(w_col_made, p.back(RING).done())
                    pool.tensor_tensor(adj_masked[k][:], adj_in[k][:], mask_all[k][:], ALU.mult).then_inc(adj_masked_made, 1)
                low_half(at(D_O2), o2_full_made, o2_full, o2_hi_made, o2_hi, o2_lo, o2_lo_made)
                p = at(D_LN1)
                if p.exists(PAIRS):
                    k = p.c % 2
                    standing_wait(pool, xn_made, p.done())
                    pool.tensor_scalar(h_full[k][:], xn[k][:], 0.0, None, ALU.max).then_inc(h_full_made, 1)
                low_half(at(D_O1), o1_full_made, o1_full, o1_hi_made, o1_hi, o1_lo, o1_lo_made)
                if p.exists(PAIRS):
                    if p.back(2).exists(PAIRS):
                        pool.wait_ge(zT_done, p.back(2).done())
                    low_half(p, h_full_made, h_full, h_hi_made, h_hi, h_lo, h_lo_made)
                    k = p.c % RING
                    pool.wait_ge(x_loaded[k], p.landed())
                    if isinstance(p.i, int) and p.c == 0:
                        pool.wait_ge(bias_loaded, 64)
                    if p.back(RING).exists(PAIRS):
                        pool.wait_ge(x1_made, p.back(RING).done())
                    pool.tensor_tensor(x_b3[k][:], x_in[k][:], b3_all[:], ALU.add).then_inc(x_b3_made, 1)

            rounds(pool, one_round)

        @block.scalar
        def _(act):
            with nc.allow_non_contiguous_dma(reason="two short bias columns"):
                act.dma_start(b1_col[:], b1.rearrange("(c h) -> h c", h=P)).then_inc(bias_loaded, 16)
                act.dma_start(b2_col[:], b2.rearrange("(c h) -> h c", h=P)).then_inc(bias_loaded, 16)
            for g in range(GB):
                act.dma_start(b3_all[:, g, :], b3.partition_broadcast(P)).then_inc(bias_loaded, 16)

            def split_weight(name):
                act.wait_ge(weight_loaded[name], 16)
                nc.scalar.activation(hi[name][:], raw[name][:], ACT.Copy).then_inc(weight_hi_made, 1)

            def prepare(u):
                if u == 1:
                    split_weight("w1")
                    split_weight("w2")
                    act.wait_ge(bias_loaded, 64)
                if u == 2:
                    act.wait_ge(qkT_transposed, 1)
                    nc.scalar.activation(qT[:], ps_qT, ACT.Copy).then_inc(qT_copied, 1)
                    split_weight("w3")
                if u == 3:
                    act.wait_ge(m_multiplied, 1)
                    nc.scalar.activation(hi["m"][:], ps_m, ACT.Copy).then_inc(weight_hi_made, 1)
                    split_weight("wv")

            def high_half(p, done, ps, high, made, n=2):
                if p.exists(PAIRS):
                    act.wait_ge(done, p.done())
                    nc.scalar.activation(high[p.c % n][:], ps, ACT.Copy).then_inc(made, 1)

            def layer_output(p, done, ps, bias, full, full_made, high, hi_made, lo_made):
                if p.exists(PAIRS):
                    k = p.c % 2
                    act.wait_ge(done, p.done())
                    if p.back(2).exists(PAIRS):
                        act.wait_ge(lo_made, p.back(2).done())
                    for c in range(C):
                        last = nc.scalar.activation(full[k][:, c], ps[:, c], ACT.Relu, bias=bias[:, c:c + 1])
                    last.then_inc(full_made, 1)
                    act.wait_ge(full_made, p.done())
                    nc.scalar.activation(high[k][:], full[k][:], ACT.Copy).then_inc(hi_made, 1)

            def one_round(at):
                high_half(at(D_ZT), zT_done, ps_zT, zT_hi, zT_hi_made)
                layer_output(at(D_O2), o2_done, ps_o2, b2_col, o2_full, o2_full_made, o2_hi, o2_hi_made, o2_lo_made)
                high_half(at(D_ADJT), aT_done, ps_aT, aT_hi, aT_hi_made, RING)
                p = at(D_H2T)
                if p.exists(PAIRS):
                    act.wait_ge(h2T_done, p.done())
                    nc.scalar.activation(h2T_hi[p.c % 2], ps_h2T, ACT.Relu).then_inc(h2T_hi_made, 1)
                layer_output(at(D_O1), o1_done, ps_o1, b1_col, o1_full, o1_full_made, o1_hi, o1_hi_made, o1_lo_made)
                p = at(D_LN1)
                if p.exists(PAIRS):
                    k = p.c % 2
                    act.wait_ge(xn_made, p.done())
                    if p.back(2).exists(PAIRS):
                        act.wait_ge(zT_done, p.back(2).done())
                        act.wait_ge(h_lo_made, p.back(2).done())
                    nc.scalar.activation(h_hi[k][:], xn[k][:], ACT.Relu).then_inc(h_hi_made, 1)
                high_half(at(D_S3), s3_done, ps_s3, s3_hi, s3_hi_made)
                p = at(D_SOFTMAX)
                if p.exists(PAIRS):
                    k = p.c % 2
                    act.wait_ge(w_row_made, p.done())
                    nc.scalar.activation(w_negmax[k][:], w_max[k][:], ACT.Copy, scale=-1.0).then_inc(w_negmax_made, 1)
                    act.wait_ge(w_negmax_made, p.done())
                    nc.scalar.activation(e_row[k][:], w_row[k][:], ACT.Exp, bias=w_negmax[k][:, 0:1],
                                         accum_out=e_sum[k][:, 0:1]).then_inc(e_made, 1)
                high_half(at(D_TT), tT_done, ps_tT, tT_hi, tT_hi_made)
                if p.exists(PAIRS):
                    act.wait_ge(e_inv_made, p.done())
                    nc.scalar.activation(p_row[k][:], e_row[k][:], ACT.Copy, scale=e_inv[k][:, 0:1]).then_inc(p_row_made, 1)
                high_half(at(D_S2), s2_done, ps_s2, s2_hi, s2_hi_made)
                p = at(D_V)
                if p.exists(PAIRS):
                    act.wait_ge(p_turned, p.done())
                    nc.scalar.activation(p_col[p.c % 2][:], ps_pcol, ACT.Copy).then_inc(p_col_made, 1)

            rounds(act, one_round, prepare)

        @block.vector
        def _(dve):
            def split_weight(n, name, src):
                dve.wait_ge(weight_hi_made, n)
                nc.vector.tensor_tensor(lo[name][:], src, hi[name][:].bitcast(F32), ALU.subtract).then_inc(weight_lo_made, 1)

            def prepare(u):
                if u == 1:
                    split_weight(1, "w1", raw["w1"][:])
                    split_weight(2, "w2", raw["w2"][:])
                if u == 2:
                    dve.wait_ge(qkT_transposed, 2)
                    nc.vector.tensor_copy(kT[:], ps_kT).then_inc(kT_copied, 1)
                    split_weight(3, "w3", raw["w3"][:])
                if u == 3:
                    split_weight(4, "m", ps_m)
                    split_weight(5, "wv", raw["wv"][:])

            def low_half(p, hi_made, ps, high, low, made, n=2):
                if p.exists(PAIRS):
                    k = p.c % n
                    dve.wait_ge(hi_made, p.done())
                    nc.vector.tensor_tensor(low[k][:], ps, high[k][:].bitcast(F32), ALU.subtract).then_inc(made, 1)

            def statistics(k, p, src, stats, stats_made, mv, mv_made):
                for g in range(GB):
                    last = nc.vector.bn_stats(stats[k][:, g, :], src[:, g, :])
                last.then_inc(stats_made, 1)
                standing_wait(dve, stats_made, p.done())
                for g in range(GB):
                    last = nc.vector.bn_aggr(mv[k][:, g, :], stats[k][:, g, :])
                last.then_inc(mv_made, 1)

            def normalise(k, dst, src, mv, rstd, made):
                for g in range(GB):
                    last = nc.vector.tensor_scalar(dst[:, g, :], src[:, g, :], mv[k][:, g, 0:1], rstd[k][:, g:g + 1],
                                                   ALU.subtract, ALU.mult)
                last.then_inc(made, 1)

            def one_round(at):
                p = at(D_LN1)
                if p.exists(PAIRS):
                    dve.wait_ge(x_loaded[p.c % RING], p.landed())
                    statistics(p.c % 2, p, x_in[p.c % RING], stats1, stats1_made, mv1, mv1_made)
                p = at(D_LN2)
                if p.exists(PAIRS):
                    dve.wait_ge(rstd2_made, p.done())
                    if p.back(2).exists(PAIRS):
                        dve.wait_ge(h2T_done, p.back(2).done())
                    normalise(p.c % 2, x1n[p.c % 2], x1[p.c % RING], mv2, rstd2, x1n_made)
                low_half(at(D_ZT), zT_hi_made, ps_zT, zT_hi, zT_lo, zT_lo_made)
                low_half(at(D_ADJT), aT_hi_made, ps_aT, aT_hi, aT_lo, aT_lo_made, RING)
                p = at(D_SC)
                if p.exists(PAIRS):
                    k = p.c % 2
                    dve.wait_ge(sc_done, p.done())
                    dve.wait_ge(adj_masked_made, p.done())
                    for g in range(GB):
                        last = nc.vector.tensor_tensor_reduce(
                            out=weighed[g][:], in0=ps_sc[:, g].rearrange("p (t n) -> p t n", t=2),
                            in1=adj_masked[p.c % RING][:, g, :].unsqueeze(1).to_broadcast([P, 2, P]), scale=1.0,
                            scalar=0.0, op0=ALU.mult, op1=ALU.add, accum_out=w_col[k][:, g:g + 1])
                    last.then_inc(w_col_made, 1)
                p = at(D_LN1)
                if p.exists(PAIRS):
                    k = p.c % 2
                    dve.wait_ge(rstd1_made, p.done())
                    if p.back(2).exists(PAIRS):
                        dve.wait_ge(h_hi_made, p.back(2).done())
                        dve.wait_ge(h_full_made, p.back(2).done())
                    normalise(k, xn[k], x_in[p.c % RING], mv1, rstd1, xn_made)
                p = at(D_H2T)
                if p.exists(PAIRS):
                    k = p.c % 2
                    dve.wait_ge(h2T_hi_made, p.done())
                    nc.vector.scalar_tensor_tensor(out=h2T_lo[k], in0=ps_h2T, scalar=0.0, in1=h2T_hi[k].bitcast(F32),
                                                   op0=ALU.max, op1=ALU.subtract).then_inc(h2T_lo_made, 1)
                p = at(D_SOFTMAX)
                if p.exists(PAIRS):
                    k = p.c % 2
                    dve.wait_ge(w_turned, p.done())
                    standing_wait(dve, row_loaded[p.c % RING], p.landed())
                    nc.vector.tensor_tensor_reduce(
                        out=w_row[k][:], in0=ps_wrow, in1=mask_row[p.c % RING][:], scale=SCALE, scalar=-3.4e38,
                        op0=ALU.mult, op1=ALU.max, accum_out=w_max[k][:, 0:1]).then_inc(w_row_made, 1)
                low_half(at(D_S3), s3_hi_made, ps_s3, s3_hi, s3_lo, s3_lo_made)
                if p.exists(PAIRS):
                    k = p.c % 2
                    dve.wait_ge(e_made, p.done())
                    nc.vector.reciprocal(e_inv[k][:], e_sum[k][:]).then_inc(e_inv_made, 1)
                low_half(at(D_TT), tT_hi_made, ps_tT, tT_hi, tT_lo, tT_lo_made)
                p = at(D_X1)
                if p.exists(PAIRS):
                    k = p.c % RING
                    dve.wait_ge(x1_done, p.done())
                    dve.wait_ge(x_b3_made, p.done())
                    if p.back(RING).exists(PAIRS):
                        dve.wait_ge(out_stored[k], p.back(RING).landed())
                    nc.vector.tensor_tensor(x1[k][:], ps_x1, x_b3[k][:], ALU.add).then_inc(x1_made, 1)
                    dve.wait_ge(x1_made, p.done())
                    statistics(p.c % 2, p, x1[k], stats2, stats2_made, mv2, mv2_made)
                low_half(at(D_S2), s2_hi_made, ps_s2, s2_hi, s2_lo, s2_lo_made)
                p = at(D_V)
                if p.exists(PAIRS):
                    dve.wait_ge(v_done, p.done())
                    dve.wait_ge(p_col_made, p.done())
                    for g in range(GB):
                        xg = x1[p.c % RING][:, g, :]
                        last = nc.vector.scalar_tensor_tensor(out=xg, in0=ps_v[:, g, :], scalar=p_col[p.c % 2][:, g:g + 1],
                                                              in1=xg, op0=ALU.mult, op1=ALU.add)
                    last.then_inc(out_made, 1)

            rounds(dve, one_round, prepare)

        @block.tensor
        def _(pe):
            pe.wait_ge(const_made, 2)

            def prepare(u):
                if u == 1:
                    pe.wait_ge(weight_loaded["qk"], 16)
                    for part, (ps, off) in enumerate(((ps_qT, 0), (ps_kT, F))):
                        for d in range(C):
                            for f in range(C):
                                last = nc.tensor.transpose(ps[:, d, f * P:(f + 1) * P],
                                                           qk_raw[:, f, off + d * P:off + (d + 1) * P], ident[:])
                        last.then_inc(qkT_transposed, 1)
                if u == 2:
                    pe.wait_ge(qT_copied, 1)
                    pe.wait_ge(kT_copied, 1)
                    for f in range(C):
                        for d in range(C):
                            last = nc.tensor.matmul(ps_m[:, f, :], qT[:, d, f * P:(f + 1) * P], kT[:, d, :],
                                                    start=d == 0, stop=d == C - 1)
                    last.then_inc(m_multiplied, 1)

            def weight_ready(p, n):
                if isinstance(p.i, int) and p.c == 0:
                    pe.wait_ge(weight_lo_made, n)

            def halves(terms, last_pass, lo_made, p, done):
                def emit(passes, first, final):
                    n = 0
                    for o, left_hi, left_lo, right_hi, right_lo in terms:
                        for which in passes:
                            left = left_lo if which == "left" else left_hi
                            right = right_lo if which == "right" else right_hi
                            n += 1
                            last = nc.tensor.matmul(o, left, right, start=first and n == 1,
                                                    stop=final and n == len(terms) * len(passes), skip_group_check=True)
                    return last

                emit(("high", "left" if last_pass == "right" else "right"), True, False)
                pe.wait_ge(lo_made, p.done())
                emit((last_pass,), False, True).then_inc(done, 1)

            def cut(t, c):
                return t[:, c * P:(c + 1) * P]

            def bank_is_out(made, p):
                if p.exists(PAIRS):
                    pe.wait_ge(made, p.done())

            def one_round(at):
                graphs_chunks = [(g, c) for g in range(GB) for c in range(C)]
                p = at(D_ZT)
                if p.exists(PAIRS):
                    k, r = p.c % 2, p.c % RING
                    pe.wait_ge(h_hi_made, p.done())
                    pe.wait_ge(aT_lo_made, p.done())
                    bank_is_out(s3_lo_made, p.back(D_S3 - D_ZT + 1))
                    halves([(ps_zT[:, c, g], cut(h_hi[k][:, g], c), cut(h_lo[k][:, g], c), aT_hi[r][:, g], aT_lo[r][:, g])
                            for g, c in graphs_chunks], "left", h_lo_made, p, zT_done)
                p = at(D_O2)
                if p.exists(PAIRS):
                    k, r = p.c % 2, p.c % RING
                    pe.wait_ge(s2_hi_made, p.done())
                    bank_is_out(tT_lo_made, p.back(D_TT - D_O2 + 1))
                    halves([(ps_o2[:, c, g], cut(s2_hi[k][:, g], c), cut(s2_lo[k][:, g], c), aT_hi[r][:, g], aT_lo[r][:, g])
                            for g, c in graphs_chunks], "left", s2_lo_made, p, o2_done)
                p = at(D_SC)
                if p.exists(PAIRS):
                    k = p.c % 2
                    pe.wait_ge(tT_hi_made, p.done())
                    bank_is_out(s2_lo_made, p.back(D_S2 - D_SC + 1))
                    for n, (g, c) in enumerate(graphs_chunks):
                        nc.tensor.matmul(ps_sc[:, g], tT_hi[k][:, c, g], h2T[k][:, c, g], start=n == 0, stop=False,
                                         skip_group_check=True)
                    pe.wait_ge(tT_lo_made, p.done())
                    for n, (g, c) in enumerate(graphs_chunks):
                        last = nc.tensor.matmul(ps_sc[:, g, 0:P], tT_lo[k][:, c, g], h2T_hi[k][:, c, g], start=False,
                                                stop=n == GB * C - 1, skip_group_check=True)
                    last.then_inc(sc_done, 1)
                p = at(D_ADJT)
                if p.exists(PAIRS):
                    r = p.c % RING
                    pe.wait_ge(adj_loaded[r], p.landed())
                    bank_is_out(x1_made, p.back(D_X1 + 1))
                    for g in range(GB):
                        last = nc.tensor.transpose(ps_aT[:, g], adj_in[r][:, g], ident[:])
                    last.then_inc(aT_done, 1)
                p = at(D_H2T)
                if p.exists(PAIRS):
                    pe.wait_ge(x1n_made, p.done())
                    bank_is_out(h2T_lo_made, p.back(1))
                    for g, c in graphs_chunks:
                        last = nc.tensor.transpose(ps_h2T[:, c, g], cut(x1n[p.c % 2][:, g], c), ident[:])
                    last.then_inc(h2T_done, 1)
                p = at(D_O1)
                if p.exists(PAIRS):
                    k = p.c % 2
                    weight_ready(p, 1)
                    pe.wait_ge(zT_hi_made, p.done())
                    bank_is_out(o1_full_made, p.back(1))
                    halves([(ps_o1[:, h], cut(hi["w1"][:, c], h), cut(lo["w1"][:, c], h), zT_hi[k][:, c], zT_lo[k][:, c])
                            for h in range(C) for c in range(C)], "right", zT_lo_made, p, o1_done)
                p = at(D_S3)
                if p.exists(PAIRS):
                    k = p.c % 2
                    weight_ready(p, 3)
                    pe.wait_ge(o2_hi_made, p.done())
                    bank_is_out(zT_lo_made, p.back(D_ZT - D_S3))
                    halves([(ps_s3[:, g], o2_hi[k][:, c, g], o2_lo[k][:, c, g], hi["w3"][:, c], lo["w3"][:, c])
                            for g, c in graphs_chunks], "left", o2_lo_made, p, s3_done)
                p = at(D_SOFTMAX)
                if p.exists(PAIRS):
                    pe.wait_ge(w_col_made, p.done())
                    bank_is_out(p_col_made, p.back(1))
                    nc.tensor.transpose(ps_wrow, w_col[p.c % 2][:], ident[:]).then_inc(w_turned, 1)
                p = at(D_TT)
                if p.exists(PAIRS):
                    k = p.c % 2
                    weight_ready(p, 4)
                    pe.wait_ge(h2T_hi_made, p.done())
                    bank_is_out(o2_full_made, p.back(D_O2 - D_TT))
                    halves([(ps_tT[:, e], cut(hi["m"][:, c], e), cut(lo["m"][:, c], e), h2T_hi[k][:, c], h2T_lo[k][:, c])
                            for e in range(C) for c in range(C)], "right", h2T_lo_made, p, tT_done)
                p = at(D_S2)
                if p.exists(PAIRS):
                    k = p.c % 2
                    weight_ready(p, 2)
                    pe.wait_ge(o1_hi_made, p.done())
                    bank_is_out(w_col_made, p.back(D_SC - D_S2))
                    halves([(ps_s2[:, g], o1_hi[k][:, c, g], o1_lo[k][:, c, g], hi["w2"][:, c], lo["w2"][:, c])
                            for g, c in graphs_chunks], "left", o1_lo_made, p, s2_done)
                p = at(D_X1)
                if p.exists(PAIRS):
                    k, r = p.c % 2, p.c % RING
                    pe.wait_ge(s3_hi_made, p.done())
                    bank_is_out(aT_lo_made, p.back(-D_X1))
                    halves([(ps_x1[:, g], aT_hi[r][:, g], aT_lo[r][:, g], s3_hi[k][:, g], s3_lo[k][:, g])
                            for g in range(GB)], "right", s3_lo_made, p, x1_done)
                p = at(D_V)
                if p.exists(PAIRS):
                    k = p.c % 2
                    weight_ready(p, 5)
                    standing_wait(pe, p_row_made, p.done())
                    nc.tensor.transpose(ps_pcol, p_row[k][:], ident[0:GB, 0:GB]).then_inc(p_turned, 1)
                    bank_is_out(out_made, p.back(1))
                    halves([(ps_v[:, g], h2T_hi[k][:, c, g], h2T_lo[k][:, c, g], hi["wv"][:, c], lo["wv"][:, c])
                            for g, c in graphs_chunks], "left", h2T_lo_made, p, v_done)

            rounds(pe, one_round, prepare)


_INS = ["x", "adj", "nodemask", "L0_gnn_W1", "L0_gnn_b1", "L0_gnn_W2", "L0_gnn_b2", "L0_gnn_W3", "L0_gnn_b3",
        "L1_gnn_Wqk", "L1_gnn_Wv"]


def kernel(**inputs):
    import numpy as np
    import concourse.bacc as bacc
    from concourse.bass_utils import run_bass_kernel_spmd

    nc = bacc.Bacc("TRN2", target_bir_lowering=False, num_devices=1)
    arrays, args = {}, []
    for name in _INS:
        a = np.ascontiguousarray(inputs[name])
        arrays[f"in_{name}"] = a
        args.append(nc.dram_tensor(f"in_{name}", a.shape, mybir.dt.from_np(a.dtype), kind="ExternalInput").ap())
    result = nc.dram_tensor("out_0", arrays["in_x"].shape, F32, kind="ExternalOutput").ap()
    gnn_kernel(nc, *args, result)
    r = run_bass_kernel_spmd(nc, [arrays], core_ids=[0])
    return r.results[0]["out_0"]
```

```python
from contextlib import ExitStack

import concourse.bass as bass
from concourse import mybir

F32 = mybir.dt.float32
F32R = mybir.dt.float32r
ALU = mybir.AluOpType
ACT = mybir.ActivationFunctionType

P = 128
GB = 2
RING = 4
EPS = 1e-5

LAST_DELAY = 5
AHEAD = 2
FIRST = 8
PREP1, PREP2, PREP3, PREP4 = 1, 2, 3, 4

AHEAD = 2


class Pair:

    def __init__(self, i, c):
        self.i, self.c = i, c

    def back(self, n):
        return Pair(self.i, self.c - n)

    def exists(self, pairs):
        return not isinstance(self.i, int) or 0 <= self.c < pairs

    def number(self):
        return self.i * RING + self.c

    def done(self):
        return self.i * RING + (self.c + 1)

    def landed(self):
        return self.i * 16 + 16 * (self.c // RING + 1)


def gnn_kernel(nc, x, adj, mask, W1, b1, W2, b2, W3, b3, Wqk, Wv, out):
    B, N, F = x.shape
    assert N == P and F == 2 * P
    C = F // P
    PAIRS = B // GB
    SCALE = float(F) ** -0.5

    LOOPS = (PAIRS - FIRST - AHEAD) // RING
    TAIL = FIRST + LOOPS * RING
    ROUNDS = PAIRS + LAST_DELAY

    with ExitStack() as ctx:
        def sb(name, shape, dt=F32):
            return ctx.enter_context(nc.sbuf_tensor(name, shape, dt))

        def ring(name, n, shape, dt=F32):
            return [sb(f"{name}{k}", shape, dt) for k in range(n)]

        def bank(name):
            return ctx.enter_context(nc.psum_tensor(name, [P, 512], F32))

        def sem(name):
            return ctx.enter_context(nc.semaphore(name))

        ident = sb("ident", [P, P])
        minus_half = sb("minus_half", [P, GB])
        b1_col = sb("b1_col", [P, C])
        b2_col = sb("b2_col", [P, C])
        b3_all = sb("b3_all", [P, GB, F])
        raw = {k: sb(f"{k}_raw", [P, C, F]) for k in ("w1", "w2", "w3", "wv")}
        qk_raw = sb("qk_raw", [P, C, 2 * F])
        qT = sb("qT", [P, C, F])
        kT = sb("kT", [P, C, F])
        hi = {k: sb(f"{k}_hi", [P, C, F], F32R) for k in ("w1", "w2", "w3", "wv", "m")}
        lo = {k: sb(f"{k}_lo", [P, C, F], F32R) for k in ("w1", "w2", "w3", "wv", "m")}

        x_in = ring("x_in", RING, [P, GB, F])
        adj_in = ring("adj_in", RING, [P, GB, P])
        mask_col = ring("mask_col", RING, [P, GB])
        mask_row = ring("mask_row", RING, [GB, P])
        x_b3 = ring("x_b3", RING, [P, GB, F])
        stats1 = ring("stats1", 2, [P, GB, 6])
        stats2 = ring("stats2", 2, [P, GB, 6])
        mv1 = ring("mv1", 2, [P, GB, 2])
        mv2 = ring("mv2", 2, [P, GB, 2])
        neg_mean1 = ring("neg_mean1", 2, [P, GB])
        neg_mean2 = ring("neg_mean2", 2, [P, GB])
        shift1 = ring("shift1", 2, [P, GB])
        shift2 = ring("shift2", 2, [P, GB])
        ve1 = ring("ve1", 2, [P, GB])
        ve2 = ring("ve2", 2, [P, GB])
        rstd1 = ring("rstd1", 2, [P, GB])
        rstd2 = ring("rstd2", 2, [P, GB])
        h_full = ring("h_full", 2, [P, GB, F])
        h_hi = ring("h_hi", 2, [P, GB, F], F32R)
        h_lo = ring("h_lo", 2, [P, GB, F], F32R)
        aT = ring("aT", RING, [P, GB, 2, P], F32R)
        aT_hi = [t[:, :, 0, :] for t in aT]
        aT_lo = [t[:, :, 1, :] for t in aT]
        zT_part = ring("zT_part", 2, [P, C, GB, P])
        zT_full = ring("zT_full", 2, [P, C, GB, P])
        zT_hi = ring("zT_hi", 2, [P, C, GB, P], F32R)
        zT_lo = ring("zT_lo", 2, [P, C, GB, P], F32R)
        o1_full = ring("o1_full", 2, [P, C, GB, P])
        o1_hi = ring("o1_hi", 2, [P, C, GB, P], F32R)
        o1_lo = ring("o1_lo", 2, [P, C, GB, P], F32R)
        s2_hi = ring("s2_hi", 2, [P, GB, F], F32R)
        s2_lo = ring("s2_lo", 2, [P, GB, F], F32R)
        o2_part = ring("o2_part", 2, [P, C, GB, P])
        o2_full = ring("o2_full", 2, [P, C, GB, P])
        o2_hi = ring("o2_hi", 2, [P, C, GB, P], F32R)
        o2_lo = ring("o2_lo", 2, [P, C, GB, P], F32R)
        s3_hi = ring("s3_hi", 2, [P, GB, F], F32R)
        s3_lo = ring("s3_lo", 2, [P, GB, F], F32R)
        x1 = ring("x1", RING, [P, GB, F])
        h2_full = ring("h2_full", 2, [P, GB, F])
        h2m_hi = ring("h2m_hi", 2, [P, GB, F], F32R)
        h2m_lo = ring("h2m_lo", 2, [P, GB, F], F32R)
        agg = ring("agg", 2, [P, GB, F])
        h2T_hi = ring("h2T_hi", 2, [P, C, GB, P], F32R)
        h2T_lo = ring("h2T_lo", 2, [P, C, GB, P], F32R)
        weighed = ring("weighed", GB, [P, F])
        w_col = ring("w_col", 2, [P, GB])
        w_row = ring("w_row", 2, [GB, P])
        w_max = ring("w_max", 2, [GB, 1])
        w_negmax = ring("w_negmax", 2, [GB, 1])
        e_row = ring("e_row", 2, [GB, P])
        e_sum = ring("e_sum", 2, [GB, 1])
        e_inv = ring("e_inv", 2, [GB, 1])
        p_row = ring("p_row", 2, [GB, P])
        p_col = ring("p_col", 2, [P, GB])

        banks = ctx.enter_context(nc.psum_tensor("banks", [P, 8, 512], F32))

        def chunk_first(b):
            return banks[:, b, :].rearrange("p (c g n) -> p c g n", c=C, g=GB)

        def graph_first(b):
            return banks[:, b, :].rearrange("p (g f) -> p g f", g=GB)

        def two_parts(b):
            return banks[:, b:b + C, :].rearrange("p c (g t n) -> p c g t n", g=GB, t=2)

        ps_zT, ps_o2 = two_parts(1), two_parts(0)
        ps_aT = banks[:, 6, 0:GB * P].rearrange("p (g n) -> p g n", g=GB)
        ps_o1, ps_h2T = chunk_first(5), chunk_first(7)
        ps_s2, ps_s3, ps_x1 = graph_first(5), graph_first(0), graph_first(2)
        ps_t, ps_agg, ps_v = graph_first(7), graph_first(4), graph_first(3)
        ps_wrow, ps_pcol = banks[0:GB, 7, 0:P], banks[:, 2, P:P + GB]
        ps_qT, ps_kT, ps_m = graph_first(4), graph_first(7), graph_first(3)
        weight_loaded = {k: sem(f"{k}_loaded") for k in ("w1", "w2", "w3", "wv", "qk")}
        bias_loaded = sem("bias_loaded")
        ident_zeroed = sem("ident_zeroed")
        const_made = sem("const_made")
        waits_passed = sem("waits_passed")
        weight_hi_made = sem("weight_hi_made")
        weight_lo_made = sem("weight_lo_made")
        qkT_transposed = sem("qkT_transposed")
        qT_copied = sem("qT_copied")
        kT_copied = sem("kT_copied")
        m_multiplied = sem("m_multiplied")
        x_loaded = [sem(f"x_loaded{k}") for k in range(RING)]
        adj_loaded = [sem(f"adj_loaded{k}") for k in range(RING)]
        mask_loaded = [sem(f"mask_loaded{k}") for k in range(RING)]
        row_loaded = [sem(f"row_loaded{k}") for k in range(RING)]
        out_stored = [sem(f"out_stored{k}") for k in range(RING)]
        x_b3_made = sem("x_b3_made")
        stats1_made = sem("stats1_made")
        stats2_made = sem("stats2_made")
        mv1_made = sem("mv1_made")
        mv2_made = sem("mv2_made")
        ve1_made = sem("ve1_made")
        ve2_made = sem("ve2_made")
        rstd1_made = sem("rstd1_made")
        rstd2_made = sem("rstd2_made")
        shift1_made = sem("shift1_made")
        shift2_made = sem("shift2_made")
        h_full_made = sem("h_full_made")
        h_hi_made = sem("h_hi_made")
        h_lo_made = sem("h_lo_made")
        aT_done = sem("aT_done")
        aT_hi_made = sem("aT_hi_made")
        aT_lo_made = sem("aT_lo_made")
        zT_done = sem("zT_done")
        zT_part_made = sem("zT_part_made")
        zT_full_made = sem("zT_full_made")
        zT_hi_made = sem("zT_hi_made")
        zT_lo_made = sem("zT_lo_made")
        o1_done = sem("o1_done")
        o1_full_made = sem("o1_full_made")
        o1_hi_made = sem("o1_hi_made")
        o1_lo_made = sem("o1_lo_made")
        s2_done = sem("s2_done")
        s2_hi_made = sem("s2_hi_made")
        s2_lo_made = sem("s2_lo_made")
        o2_done = sem("o2_done")
        o2_part_made = sem("o2_part_made")
        o2_full_made = sem("o2_full_made")
        o2_hi_made = sem("o2_hi_made")
        o2_lo_made = sem("o2_lo_made")
        s3_done = sem("s3_done")
        s3_hi_made = sem("s3_hi_made")
        s3_lo_made = sem("s3_lo_made")
        x1_done = sem("x1_done")
        x1_made = sem("x1_made")
        h2T_done = sem("h2T_done")
        h2T_hi_made = sem("h2T_hi_made")
        h2T_lo_made = sem("h2T_lo_made")
        w_col_made = sem("w_col_made")
        w_turned = sem("w_turned")
        w_row_made = sem("w_row_made")
        w_negmax_made = sem("w_negmax_made")
        e_made = sem("e_made")
        e_inv_made = sem("e_inv_made")
        p_row_made = sem("p_row_made")
        p_turned = sem("p_turned")
        p_col_made = sem("p_col_made")
        v_done = sem("v_done")
        h2_full_made = sem("h2_full_made")
        h2m_hi_made = sem("h2m_hi_made")
        h2m_lo_made = sem("h2m_lo_made")
        agg_done = sem("agg_done")
        agg_made = sem("agg_made")
        t_done = sem("t_done")
        out_made = sem("out_made")

        def standing_wait(eng, made, count):
            eng.wait_ge(made, count)
            eng.sem_inc(waits_passed, 1)

        def free(eng, read, p):
            if p.exists(PAIRS):
                eng.wait_ge(read, p.done())

        def rounds(eng, one_round, prepare=lambda u: None):
            for u in range(FIRST):
                prepare(u)
                one_round(lambda n: Pair(0, u - n))
            with eng.Fori(0, LOOPS, 1) as i:
                for j in range(RING):
                    one_round(lambda n: Pair(i, FIRST + j - n))
            for u in range(TAIL, ROUNDS):
                one_round(lambda n: Pair(0, u - n))

        block = ctx.enter_context(nc.Block())

        @block.sync
        def _(sp):
            def load(p):
                if not p.exists(PAIRS):
                    return
                k, old, first = p.c % RING, p.back(RING), p.number() * GB
                again = old.exists(PAIRS)
                if again:
                    sp.wait_ge(h_full_made, old.done())
                    sp.wait_ge(x_b3_made, old.done())
                sp.dma_start(x_in[k][:], x[bass.ds(first, GB)].rearrange("g n f -> n g f")).then_inc(x_loaded[k], 16)
                if again:
                    sp.wait_ge(aT_done, old.done())
                sp.dma_start(adj_in[k][:], adj[bass.ds(first, GB)].rearrange("g n m -> n g m")).then_inc(adj_loaded[k], 16)

            def load_mask(p):
                if p.exists(PAIRS):
                    k, old = p.c % RING, p.back(RING)
                    rows = mask[bass.ds(p.number() * GB, GB)]
                    if old.exists(PAIRS):
                        sp.wait_ge(h2m_lo_made, old.done())
                        sp.wait_ge(w_row_made, old.done())
                    with nc.allow_non_contiguous_dma(reason="two short mask columns"):
                        sp.dma_start(mask_col[k][:], rows.rearrange("g n -> n g")).then_inc(mask_loaded[k], 16)
                    sp.dma_start(mask_row[k][:], rows).then_inc(row_loaded[k], 16)

            def store(p):
                if p.exists(PAIRS):
                    k = p.c % RING
                    sp.wait_ge(out_made, p.done())
                    sp.dma_start(out[bass.ds(p.number() * GB, GB)].rearrange("g n f -> n g f"), x1[k][:]).then_inc(out_stored[k], 16)

            def load_weight(name, dst, src):
                sp.dma_start(dst[:], src.rearrange("(c f) h -> f c h", f=P)).then_inc(weight_loaded[name], 16)

            load(Pair(0, 0))
            load_weight("w1", raw["w1"], W1)
            load(Pair(0, 1))
            load_weight("w2", raw["w2"], W2)
            load_weight("qk", qk_raw, Wqk)
            load_weight("w3", raw["w3"], W3)
            load_weight("wv", raw["wv"], Wv)

            def one_round(at):
                load(at(-AHEAD))
                load_mask(at(1))
                store(at(4))

            rounds(sp, one_round)
            for k in range(RING):
                sp.wait_ge(out_stored[k], 16 * (PAIRS // RING))

        @block.gpsimd
        def _(pool):
            pool.memset(ident[:], 0.0).then_inc(ident_zeroed, 1)
            pool.memset(minus_half[:], -0.5).then_inc(const_made, 1)
            pool.wait_ge(ident_zeroed, 1)
            pool.affine_select(out=ident[:], in_=ident[:], compare_op=ALU.not_equal, fill=1.0, base=0,
                               pattern=[[-1, P]], channel_multiplier=1).then_inc(const_made, 1)
            pool.wait_ge(const_made, 2)

            def minus_mean_and_ve(p, mv_made, mv, neg_mean, ve, ve_made):
                k = p.c % 2
                standing_wait(pool, mv_made, p.done())
                pool.tensor_scalar(ve[k][:], mv[k][:, :, 1], EPS, None, ALU.add).then_inc(ve_made, 1)
                pool.tensor_scalar(neg_mean[k][:], mv[k][:, :, 0], -1.0, None, ALU.mult).then_inc(ve_made, 1)

            def power(p, ve_made, ve, rstd, rstd_made):
                k = p.c % 2
                pool.wait_ge(ve_made, p.done() + p.done())
                pool.tensor_tensor(rstd[k][:], ve[k][:], minus_half[:], ALU.pow).then_inc(rstd_made, 1)

            def times_mean(p, rstd_made, rstd, neg_mean, shift, shift_made):
                k = p.c % 2
                pool.wait_ge(rstd_made, p.done())
                pool.tensor_tensor(shift[k][:], neg_mean[k][:], rstd[k][:], ALU.mult).then_inc(shift_made, 1)

            def variance1(p):
                if not p.exists(PAIRS):
                    return
                minus_mean_and_ve(p, mv1_made, mv1, neg_mean1, ve1, ve1_made)

            def power1(p):
                if not p.exists(PAIRS):
                    return
                power(p, ve1_made, ve1, rstd1, rstd1_made)

            def shift1_(p):
                if not p.exists(PAIRS):
                    return
                times_mean(p, rstd1_made, rstd1, neg_mean1, shift1, shift1_made)

            def zT_low(p):
                if not p.exists(PAIRS):
                    return
                k = p.c % 2
                pool.wait_ge(zT_hi_made, p.done())
                pool.tensor_tensor(zT_lo[k][:], zT_full[k][:], zT_hi[k][:].bitcast(F32), ALU.subtract).then_inc(zT_lo_made, 1)

            def add_b3(p):
                if not p.exists(PAIRS):
                    return
                r = p.c % RING
                pool.wait_ge(x_loaded[r], p.landed())
                if isinstance(p.i, int) and p.c == 0:
                    pool.wait_ge(bias_loaded, 64)
                pool.tensor_tensor(x_b3[r][:], x_in[r][:], b3_all[:], ALU.add).then_inc(x_b3_made, 1)

            def variance2(p):
                if not p.exists(PAIRS):
                    return
                minus_mean_and_ve(p, mv2_made, mv2, neg_mean2, ve2, ve2_made)

            def power2(p):
                if not p.exists(PAIRS):
                    return
                power(p, ve2_made, ve2, rstd2, rstd2_made)

            def shift2_(p):
                if not p.exists(PAIRS):
                    return
                times_mean(p, rstd2_made, rstd2, neg_mean2, shift2, shift2_made)

            def o1_low(p):
                if not p.exists(PAIRS):
                    return
                k = p.c % 2
                pool.wait_ge(o1_hi_made, p.done())
                pool.tensor_tensor(o1_lo[k][:], o1_full[k][:], o1_hi[k][:].bitcast(F32), ALU.subtract).then_inc(o1_lo_made, 1)

            def one_round(at):
                variance1(at(2))
                power1(at(2))
                shift1_(at(2))
                zT_low(at(3))
                add_b3(at(3))
                variance2(at(5))
                power2(at(5))
                shift2_(at(5))
                o1_low(at(3))

            rounds(pool, one_round)

        @block.scalar
        def _(act):
            with nc.allow_non_contiguous_dma(reason="two short bias columns"):
                act.dma_start(b1_col[:], b1.rearrange("(c h) -> h c", h=P)).then_inc(bias_loaded, 16)
                act.dma_start(b2_col[:], b2.rearrange("(c h) -> h c", h=P)).then_inc(bias_loaded, 16)
            for g in range(GB):
                act.dma_start(b3_all[:, g, :], b3.partition_broadcast(P)).then_inc(bias_loaded, 16)

            def split_weight(name):
                act.wait_ge(weight_loaded[name], 16)
                nc.scalar.activation(hi[name][:], raw[name][:], ACT.Copy).then_inc(weight_hi_made, 1)

            def prepare(u):
                if u == PREP1:
                    act.wait_ge(bias_loaded, 64)
                    split_weight("w1")
                if u == PREP2:
                    split_weight("w2")
                    act.wait_ge(qkT_transposed, 1)
                    nc.scalar.activation(qT[:], ps_qT, ACT.Copy).then_inc(qT_copied, 1)
                    split_weight("w3")
                if u == PREP4:
                    act.wait_ge(m_multiplied, 1)
                    nc.scalar.activation(hi["m"][:], ps_m, ACT.Copy).then_inc(weight_hi_made, 1)
                    split_weight("wv")

            def scaled(p, src, rstd, shift, shift_made, dst, made):
                k = p.c % 2
                act.wait_ge(shift_made, p.done())
                for g in range(GB):
                    last = nc.scalar.activation(dst[k][:, g], src[p.c % RING][:, g], ACT.Relu, bias=shift[k][:, g:g + 1],
                                                scale=rstd[k][:, g:g + 1])
                last.then_inc(made, 1)

            def s2_high(p):
                if not p.exists(PAIRS):
                    return
                k = p.c % 2
                act.wait_ge(s2_done, p.done())
                nc.scalar.activation(s2_hi[k][:], ps_s2, ACT.Copy).then_inc(s2_hi_made, 1)

            def zT_high(p):
                if not p.exists(PAIRS):
                    return
                k = p.c % 2
                act.wait_ge(zT_full_made, p.done())
                nc.scalar.activation(zT_hi[k][:], zT_full[k][:], ACT.Copy).then_inc(zT_hi_made, 1)

            def h2T_high(p):
                if not p.exists(PAIRS):
                    return
                k = p.c % 2
                act.wait_ge(h2T_done, p.done())
                nc.scalar.activation(h2T_hi[k][:], ps_h2T, ACT.Copy).then_inc(h2T_hi_made, 1)

            def softmax_row(p):
                if not p.exists(PAIRS):
                    return
                k = p.c % 2
                act.wait_ge(e_inv_made, p.done())
                nc.scalar.activation(p_row[k][:], e_row[k][:], ACT.Copy, scale=e_inv[k][:, 0:1]).then_inc(p_row_made, 1)

            def h_whole(p):
                if not p.exists(PAIRS):
                    return
                scaled(p, x_in, rstd1, shift1, shift1_made, h_full, h_full_made)

            def aT_high(p):
                if not p.exists(PAIRS):
                    return
                r = p.c % RING
                free(act, agg_done, p.back(4))
                act.wait_ge(aT_done, p.done())
                nc.scalar.activation(aT_hi[r], ps_aT, ACT.Copy).then_inc(aT_hi_made, 1)

            def softmax_col(p):
                if not p.exists(PAIRS):
                    return
                k = p.c % 2
                act.wait_ge(p_turned, p.done())
                nc.scalar.activation(p_col[k][:], ps_pcol, ACT.Copy).then_inc(p_col_made, 1)

            def copy_agg(p):
                if not p.exists(PAIRS):
                    return
                k = p.c % 2
                act.wait_ge(agg_done, p.done())
                nc.scalar.activation(agg[k][:], ps_agg, ACT.Copy).then_inc(agg_made, 1)

            def o2_lows_part(p):
                if not p.exists(PAIRS):
                    return
                k = p.c % 2
                act.wait_ge(o2_done, p.done())
                for c in range(C):
                    last = nc.scalar.activation(o2_part[k][:, c], ps_o2[:, c, :, 1], ACT.Identity, bias=b2_col[:, c:c + 1])
                last.then_inc(o2_part_made, 1)

            def h_high(p):
                if not p.exists(PAIRS):
                    return
                k = p.c % 2
                act.wait_ge(h_full_made, p.done())
                nc.scalar.activation(h_hi[k][:], h_full[k][:], ACT.Copy).then_inc(h_hi_made, 1)

            def o1_whole(p):
                if not p.exists(PAIRS):
                    return
                k = p.c % 2
                act.wait_ge(o1_done, p.done())
                for c in range(C):
                    last = nc.scalar.activation(o1_full[k][:, c], ps_o1[:, c], ACT.Relu, bias=b1_col[:, c:c + 1])
                last.then_inc(o1_full_made, 1)

            def o2_high(p):
                if not p.exists(PAIRS):
                    return
                k = p.c % 2
                act.wait_ge(o2_full_made, p.done())
                nc.scalar.activation(o2_hi[k][:], o2_full[k][:], ACT.Relu).then_inc(o2_hi_made, 1)

            def o1_high(p):
                if not p.exists(PAIRS):
                    return
                k = p.c % 2
                act.wait_ge(o1_full_made, p.done())
                nc.scalar.activation(o1_hi[k][:], o1_full[k][:], ACT.Copy).then_inc(o1_hi_made, 1)

            def h2_whole(p):
                if not p.exists(PAIRS):
                    return
                scaled(p, x1, rstd2, shift2, shift2_made, h2_full, h2_full_made)

            def zT_lows_part(p):
                if not p.exists(PAIRS):
                    return
                k = p.c % 2
                act.wait_ge(zT_done, p.done())
                nc.scalar.activation(zT_part[k][:], ps_zT[:, :, :, 1], ACT.Copy).then_inc(zT_part_made, 1)

            def h2m_high(p):
                if not p.exists(PAIRS):
                    return
                k, r = p.c % 2, p.c % RING
                act.wait_ge(mask_loaded[r], p.landed())
                act.wait_ge(h2_full_made, p.done())
                for g in range(GB):
                    last = nc.scalar.activation(h2m_hi[k][:, g], h2_full[k][:, g], ACT.Copy, scale=mask_col[r][:, g:g + 1])
                last.then_inc(h2m_hi_made, 1)

            def s3_high(p):
                if not p.exists(PAIRS):
                    return
                k = p.c % 2
                act.wait_ge(s3_done, p.done())
                nc.scalar.activation(s3_hi[k][:], ps_s3, ACT.Copy).then_inc(s3_hi_made, 1)

            def negative_max(p):
                if not p.exists(PAIRS):
                    return
                k = p.c % 2
                act.wait_ge(w_row_made, p.done())
                nc.scalar.activation(w_negmax[k][:], w_max[k][:], ACT.Copy, scale=-1.0).then_inc(w_negmax_made, 1)

            def exp_w(p):
                if not p.exists(PAIRS):
                    return
                k = p.c % 2
                act.wait_ge(w_negmax_made, p.done())
                nc.scalar.activation(e_row[k][:], w_row[k][:], ACT.Exp, bias=w_negmax[k][:, 0:1],
                                     accum_out=e_sum[k][:, 0:1]).then_inc(e_made, 1)

            def one_round(at):
                s2_high(at(2))
                zT_high(at(1))
                h2T_high(at(4))
                softmax_row(at(5))
                h_whole(at(0))
                aT_high(at(0))
                softmax_col(at(5))
                copy_agg(at(4))
                o2_lows_part(at(2))
                h_high(at(0))
                o1_whole(at(1))
                o2_high(at(2))
                o1_high(at(1))
                h2_whole(at(3))
                zT_lows_part(at(0))
                h2m_high(at(3))
                s3_high(at(2))
                negative_max(at(4))
                exp_w(at(4))

            rounds(act, one_round, prepare)

        @block.vector
        def _(dve):
            def split_weight(n, name, src):
                dve.wait_ge(weight_hi_made, n)
                nc.vector.tensor_tensor(lo[name][:], src, hi[name][:].bitcast(F32), ALU.subtract).then_inc(weight_lo_made, 1)

            def prepare(u):
                if u == PREP1:
                    split_weight(1, "w1", raw["w1"][:])
                if u == PREP2:
                    split_weight(2, "w2", raw["w2"][:])
                    dve.wait_ge(qkT_transposed, 2)
                    nc.vector.tensor_copy(kT[:], ps_kT).then_inc(kT_copied, 1)
                    split_weight(3, "w3", raw["w3"][:])
                if u == PREP4:
                    split_weight(4, "m", ps_m)
                    split_weight(5, "wv", raw["wv"][:])

            def statistics(p, src, stats, stats_made):
                for g in range(GB):
                    last = nc.vector.bn_stats(stats[p.c % 2][:, g, :], src[:, g, :])
                last.then_inc(stats_made, 1)

            def mean_and_variance(p, stats_made, stats, mv, mv_made):
                k = p.c % 2
                standing_wait(dve, stats_made, p.done())
                for g in range(GB):
                    last = nc.vector.bn_aggr(mv[k][:, g, :], stats[k][:, g, :])
                last.then_inc(mv_made, 1)

            def add_parts(p, part_made, ps, part, full, made):
                k = p.c % 2
                dve.wait_ge(part_made, p.done())
                nc.vector.tensor_tensor(full[k][:], ps[:, :, :, 0], part[k][:], ALU.add).then_inc(made, 1)

            def statistics1(p):
                if not p.exists(PAIRS):
                    return
                r = p.c % RING
                dve.wait_ge(x_loaded[r], p.landed())
                statistics(p, x_in[r], stats1, stats1_made)

            def mean_variance1(p):
                if not p.exists(PAIRS):
                    return
                mean_and_variance(p, stats1_made, stats1, mv1, mv1_made)

            def zT_whole(p):
                if not p.exists(PAIRS):
                    return
                add_parts(p, zT_part_made, ps_zT, zT_part, zT_full, zT_full_made)

            def mask_weights(p):
                if not p.exists(PAIRS):
                    return
                k, r = p.c % 2, p.c % RING
                dve.wait_ge(w_turned, p.done())
                standing_wait(dve, row_loaded[r], p.landed())
                nc.vector.tensor_tensor_reduce(out=w_row[k][:], in0=ps_wrow, in1=mask_row[r][:], scale=SCALE, scalar=-3.4e38,
                                               op0=ALU.mult, op1=ALU.max, accum_out=w_max[k][:, 0:1]).then_inc(w_row_made, 1)

            def s3_low(p):
                if not p.exists(PAIRS):
                    return
                k = p.c % 2
                dve.wait_ge(s3_hi_made, p.done())
                nc.vector.tensor_tensor(s3_lo[k][:], ps_s3, s3_hi[k][:].bitcast(F32), ALU.subtract).then_inc(s3_lo_made, 1)

            def h2m_low(p):
                if not p.exists(PAIRS):
                    return
                k, r = p.c % 2, p.c % RING
                dve.wait_ge(h2m_hi_made, p.done())
                for g in range(GB):
                    last = nc.vector.scalar_tensor_tensor(out=h2m_lo[k][:, g], in0=h2_full[k][:, g], scalar=mask_col[r][:, g:g + 1],
                                                          in1=h2m_hi[k][:, g].bitcast(F32), op0=ALU.mult, op1=ALU.subtract)
                last.then_inc(h2m_lo_made, 1)

            def inverse_sum(p):
                if not p.exists(PAIRS):
                    return
                k = p.c % 2
                dve.wait_ge(e_made, p.done())
                nc.vector.reciprocal(e_inv[k][:], e_sum[k][:]).then_inc(e_inv_made, 1)

            def s2_low(p):
                if not p.exists(PAIRS):
                    return
                k = p.c % 2
                dve.wait_ge(s2_hi_made, p.done())
                nc.vector.tensor_tensor(s2_lo[k][:], ps_s2, s2_hi[k][:].bitcast(F32), ALU.subtract).then_inc(s2_lo_made, 1)

            def residual(p):
                if not p.exists(PAIRS):
                    return
                r = p.c % RING
                dve.wait_ge(x1_done, p.done())
                dve.wait_ge(x_b3_made, p.done())
                if p.back(RING).exists(PAIRS):
                    dve.wait_ge(out_stored[r], p.back(RING).landed())
                nc.vector.tensor_tensor(x1[r][:], ps_x1, x_b3[r][:], ALU.add).then_inc(x1_made, 1)

            def h2T_low(p):
                if not p.exists(PAIRS):
                    return
                k = p.c % 2
                dve.wait_ge(h2T_hi_made, p.done())
                nc.vector.tensor_tensor(h2T_lo[k][:], ps_h2T, h2T_hi[k][:].bitcast(F32), ALU.subtract).then_inc(h2T_lo_made, 1)

            def statistics2(p):
                if not p.exists(PAIRS):
                    return
                r = p.c % RING
                dve.wait_ge(x1_made, p.done())
                statistics(p, x1[r], stats2, stats2_made)

            def aT_low(p):
                if not p.exists(PAIRS):
                    return
                r = p.c % RING
                dve.wait_ge(aT_hi_made, p.done())
                nc.vector.tensor_tensor(aT_lo[r], ps_aT, aT_hi[r].bitcast(F32), ALU.subtract).then_inc(aT_lo_made, 1)

            def mean_variance2(p):
                if not p.exists(PAIRS):
                    return
                mean_and_variance(p, stats2_made, stats2, mv2, mv2_made)

            def output(p):
                if not p.exists(PAIRS):
                    return
                k, r = p.c % 2, p.c % RING
                dve.wait_ge(v_done, p.done())
                dve.wait_ge(p_col_made, p.done())
                for g in range(GB):
                    last = nc.vector.scalar_tensor_tensor(out=x1[r][:, g], in0=ps_v[:, g], scalar=p_col[k][:, g:g + 1],
                                                          in1=x1[r][:, g], op0=ALU.mult, op1=ALU.add)
                last.then_inc(out_made, 1)

            def o2_whole(p):
                if not p.exists(PAIRS):
                    return
                add_parts(p, o2_part_made, ps_o2, o2_part, o2_full, o2_full_made)

            def h_low(p):
                if not p.exists(PAIRS):
                    return
                k = p.c % 2
                dve.wait_ge(h_hi_made, p.done())
                nc.vector.tensor_tensor(h_lo[k][:], h_full[k][:], h_hi[k][:].bitcast(F32), ALU.subtract).then_inc(h_lo_made, 1)

            def weights(p):
                if not p.exists(PAIRS):
                    return
                k = p.c % 2
                dve.wait_ge(t_done, p.done())
                dve.wait_ge(agg_made, p.done())
                for g in range(GB):
                    last = nc.vector.tensor_tensor_reduce(
                        out=weighed[g][:], in0=ps_t[:, g], in1=agg[k][:, g], scale=1.0, scalar=0.0, op0=ALU.mult, op1=ALU.add,
                        accum_out=w_col[k][:, g:g + 1])
                last.then_inc(w_col_made, 1)

            def o2_low(p):
                if not p.exists(PAIRS):
                    return
                k = p.c % 2
                dve.wait_ge(o2_hi_made, p.done())
                nc.vector.scalar_tensor_tensor(out=o2_lo[k][:], in0=o2_full[k][:], scalar=0.0, in1=o2_hi[k][:].bitcast(F32),
                                               op0=ALU.max, op1=ALU.subtract).then_inc(o2_lo_made, 1)

            def one_round(at):
                statistics1(at(0))
                mean_variance1(at(0))
                zT_whole(at(1))
                mask_weights(at(5))
                s3_low(at(3))
                h2m_low(at(4))
                inverse_sum(at(5))
                s2_low(at(2))
                residual(at(3))
                h2T_low(at(4))
                statistics2(at(3))
                aT_low(at(0))
                mean_variance2(at(3))
                output(at(5))
                o2_whole(at(2))
                h_low(at(0))
                weights(at(4))
                o2_low(at(2))

            rounds(dve, one_round, prepare)

        @block.tensor
        def _(pe):
            pe.wait_ge(const_made, 2)

            def prepare(u):
                if u == PREP2:
                    pe.wait_ge(weight_loaded["qk"], 16)
                    for part, (ps, off) in enumerate(((ps_qT, 0), (ps_kT, F))):
                        for d in range(C):
                            for f in range(C):
                                last = nc.tensor.transpose(ps[:, d, f * P:(f + 1) * P],
                                                           qk_raw[:, f, off + d * P:off + (d + 1) * P], ident[:])
                        last.then_inc(qkT_transposed, 1)
                if u == PREP3:
                    pe.wait_ge(qT_copied, 1)
                    pe.wait_ge(kT_copied, 1)
                    for f in range(C):
                        for d in range(C):
                            last = nc.tensor.matmul(ps_m[:, f, :], qT[:, d, f * P:(f + 1) * P], kT[:, d, :],
                                                    start=d == 0, stop=d == C - 1)
                    last.then_inc(m_multiplied, 1)
                if u == PREP4:
                    pe.wait_ge(weight_lo_made, 4)

            def weight_ready(p, n):
                if isinstance(p.i, int) and p.c == 0:
                    pe.wait_ge(weight_lo_made, n)

            def bank_free(p, last_user, *others):
                users = (last_user,) + (others if isinstance(p.i, int) else ())
                for read, n in users:
                    free(pe, read, p.back(n))

            def halves(terms, last_pass, lo_made, p, done):
                def emit(passes, first, final):
                    n = 0
                    for o, left_hi, left_lo, right_hi, right_lo in terms:
                        for which in passes:
                            left = left_lo if which == "left" else left_hi
                            right = right_lo if which == "right" else right_hi
                            n += 1
                            last = nc.tensor.matmul(o, left, right, start=first and n == 1,
                                                    stop=final and n == len(terms) * len(passes), skip_group_check=True)
                    return last

                emit(("high", "left" if last_pass == "right" else "right"), True, False)
                pe.wait_ge(lo_made, p.done())
                emit((last_pass,), False, True).then_inc(done, 1)

            def cut(t, c):
                return t[:, c * P:(c + 1) * P]

            def with_adj(ps, left_hi, left_lo, r, lo_made, p, done):
                for c in range(C):
                    for g in range(GB):
                        nc.tensor.matmul(ps[:, c, g], cut(left_hi[:, g], c), aT[r][:, g], start=g == 0, stop=False,
                                         skip_group_check=True)
                pe.wait_ge(lo_made, p.done())
                for c in range(C):
                    for g in range(GB):
                        last = nc.tensor.matmul(ps[:, c, g, 0], cut(left_lo[:, g], c), aT_hi[r][:, g], start=False,
                                                stop=g == GB - 1, skip_group_check=True)
                last.then_inc(done, 1)

            graphs_chunks = [(g, c) for g in range(GB) for c in range(C)]

            def product_s2(p):
                if not p.exists(PAIRS):
                    return
                k = p.c % 2
                weight_ready(p, 2)
                pe.wait_ge(o1_hi_made, p.done())
                bank_free(p, (o1_full_made, 0), (s2_lo_made, 1))
                halves([(ps_s2[:, g], o1_hi[k][:, c, g], o1_lo[k][:, c, g], hi["w2"][:, c], lo["w2"][:, c])
                        for g, c in graphs_chunks], "left", o1_lo_made, p, s2_done)

            def transpose_h2(p):
                if not p.exists(PAIRS):
                    return
                k = p.c % 2
                pe.wait_ge(h2_full_made, p.done())
                bank_free(p, (w_row_made, 1), (w_col_made, 1), (h2T_lo_made, 1))
                for g, c in graphs_chunks:
                    last = nc.tensor.transpose(ps_h2T[:, c, g], cut(h2_full[k][:, g], c), ident[:])
                last.then_inc(h2T_done, 1)

            def transpose_adj(p):
                if not p.exists(PAIRS):
                    return
                r = p.c % RING
                pe.wait_ge(adj_loaded[r], p.landed())
                bank_free(p, (aT_lo_made, 1))
                for g in range(GB):
                    last = nc.tensor.transpose(ps_aT[:, g], adj_in[r][:, g], ident[:])
                last.then_inc(aT_done, 1)

            def product_x1(p):
                if not p.exists(PAIRS):
                    return
                k, r = p.c % 2, p.c % RING
                pe.wait_ge(s3_hi_made, p.done())
                bank_free(p, (zT_full_made, -2), (p_col_made, 3), (x1_made, 1))
                halves([(ps_x1[:, g], aT_hi[r][:, g], aT_lo[r][:, g], s3_hi[k][:, g], s3_lo[k][:, g]) for g in range(GB)],
                       "right", s3_lo_made, p, x1_done)

            def product_agg(p):
                if not p.exists(PAIRS):
                    return
                k, r = p.c % 2, p.c % RING
                pe.wait_ge(h2m_hi_made, p.done())
                bank_free(p, (agg_made, 1))
                halves([(ps_agg[:, g], aT_hi[r][:, g], aT_lo[r][:, g], h2m_hi[k][:, g], h2m_lo[k][:, g]) for g in range(GB)],
                       "right", h2m_lo_made, p, agg_done)

            def product_o2(p):
                if not p.exists(PAIRS):
                    return
                k, r = p.c % 2, p.c % RING
                pe.wait_ge(s2_hi_made, p.done())
                bank_free(p, (s3_lo_made, 1), (o2_full_made, 1))
                bank_free(p, (zT_full_made, -1), (o2_full_made, 1))
                with_adj(ps_o2, s2_hi[k], s2_lo[k], r, s2_lo_made, p, o2_done)

            def turn_p(p):
                if not p.exists(PAIRS):
                    return
                k = p.c % 2
                bank_free(p, (x1_made, -2), (zT_full_made, -4), (p_col_made, 1))
                standing_wait(pe, p_row_made, p.done())
                nc.tensor.transpose(ps_pcol, p_row[k][:], ident[0:GB, 0:GB]).then_inc(p_turned, 1)

            def product_o1(p):
                if not p.exists(PAIRS):
                    return
                k = p.c % 2
                weight_ready(p, 1)
                pe.wait_ge(zT_hi_made, p.done())
                bank_free(p, (s2_lo_made, 1), (o1_full_made, 1))
                halves([(ps_o1[:, h], cut(hi["w1"][:, c], h), cut(lo["w1"][:, c], h), zT_hi[k][:, c], zT_lo[k][:, c])
                        for h in range(C) for c in range(C)], "right", zT_lo_made, p, o1_done)

            def product_t(p):
                if not p.exists(PAIRS):
                    return
                k = p.c % 2
                weight_ready(p, 4)
                pe.wait_ge(h2T_hi_made, p.done())
                bank_free(p, (h2T_lo_made, 0), (w_row_made, 1), (w_col_made, 1))
                halves([(ps_t[:, g], h2T_hi[k][:, c, g], h2T_lo[k][:, c, g], hi["m"][:, c], lo["m"][:, c])
                        for g, c in graphs_chunks], "left", h2T_lo_made, p, t_done)

            def product_v(p):
                if not p.exists(PAIRS):
                    return
                k = p.c % 2
                weight_ready(p, 5)
                bank_free(p, (out_made, 1))
                halves([(ps_v[:, g], h2T_hi[k][:, c, g], h2T_lo[k][:, c, g], hi["wv"][:, c], lo["wv"][:, c])
                        for g, c in graphs_chunks], "left", h2T_lo_made, p, v_done)

            def product_zT(p):
                if not p.exists(PAIRS):
                    return
                k, r = p.c % 2, p.c % RING
                pe.wait_ge(h_hi_made, p.done())
                pe.wait_ge(aT_lo_made, p.done())
                bank_free(p, (o2_full_made, 2), (zT_full_made, 1))
                bank_free(p, (p_col_made, 5), (x1_made, 3), (zT_full_made, 1))
                with_adj(ps_zT, h_hi[k], h_lo[k], r, h_lo_made, p, zT_done)

            def product_s3(p):
                if not p.exists(PAIRS):
                    return
                k = p.c % 2
                weight_ready(p, 3)
                pe.wait_ge(o2_hi_made, p.done())
                bank_free(p, (o2_full_made, 0), (s3_lo_made, 1))
                halves([(ps_s3[:, g], o2_hi[k][:, c, g], o2_lo[k][:, c, g], hi["w3"][:, c], lo["w3"][:, c])
                        for g, c in graphs_chunks], "left", o2_lo_made, p, s3_done)

            def turn_w(p):
                if not p.exists(PAIRS):
                    return
                k = p.c % 2
                pe.wait_ge(w_col_made, p.done())
                bank_free(p, (w_col_made, 0), (h2T_lo_made, 0), (w_row_made, 1))
                nc.tensor.transpose(ps_wrow, w_col[k][:], ident[:]).then_inc(w_turned, 1)

            def one_round(at):
                product_s2(at(2))
                transpose_h2(at(4))
                transpose_adj(at(0))
                product_x1(at(3))
                product_agg(at(4))
                product_o2(at(2))
                turn_p(at(5))
                product_o1(at(1))
                product_t(at(4))
                product_v(at(4))
                product_zT(at(0))
                product_s3(at(2))
                turn_w(at(4))

            rounds(pe, one_round, prepare)


_INS = ["x", "adj", "nodemask", "L0_gnn_W1", "L0_gnn_b1", "L0_gnn_W2", "L0_gnn_b2", "L0_gnn_W3", "L0_gnn_b3",
        "L1_gnn_Wqk", "L1_gnn_Wv"]


def kernel(**inputs):
    import numpy as np
    import concourse.bacc as bacc
    from concourse.bass_utils import run_bass_kernel_spmd

    nc = bacc.Bacc("TRN2", target_bir_lowering=False, num_devices=1)
    arrays, args = {}, []
    for name in _INS:
        a = np.ascontiguousarray(inputs[name])
        arrays[f"in_{name}"] = a
        args.append(nc.dram_tensor(f"in_{name}", a.shape, mybir.dt.from_np(a.dtype), kind="ExternalInput").ap())
    result = nc.dram_tensor("out_0", arrays["in_x"].shape, F32, kind="ExternalOutput").ap()
    gnn_kernel(nc, *args, result)
    r = run_bass_kernel_spmd(nc, [arrays], core_ids=[0])
    return r.results[0]["out_0"]
```

```python
from contextlib import ExitStack

import concourse.bass as bass
from concourse import mybir

F32 = mybir.dt.float32
F32R = mybir.dt.float32r
ALU = mybir.AluOpType
ACT = mybir.ActivationFunctionType

P = 128
GB = 2
RING = 4
EPS = 1e-5

LAST_DELAY = 5
FIRST = 9
AHEAD = 2


class Pair:

    def __init__(self, i, c):
        self.i, self.c = i, c

    def back(self, n):
        return Pair(self.i, self.c - n)

    def exists(self, pairs):
        return not isinstance(self.i, int) or 0 <= self.c < pairs

    def number(self):
        return self.i * RING + self.c

    def done(self):
        return self.i * RING + (self.c + 1)

    def landed(self):
        return self.i * 16 + 16 * (self.c // RING + 1)


def gnn_kernel(nc, x, adj, mask, W1, b1, W2, b2, W3, b3, Wqk, Wv, out):
    B, N, F = x.shape
    assert N == P and F == 2 * P
    C = F // P
    PAIRS = B // GB
    SCALE = float(F) ** -0.5

    LOOPS = (PAIRS - FIRST - AHEAD) // RING
    TAIL = FIRST + LOOPS * RING
    ROUNDS = PAIRS + LAST_DELAY

    with ExitStack() as ctx:
        def sb(name, shape, dt=F32):
            return ctx.enter_context(nc.sbuf_tensor(name, shape, dt))

        def ring(name, n, shape, dt=F32):
            return [sb(f"{name}{k}", shape, dt) for k in range(n)]

        def bank(name):
            return ctx.enter_context(nc.psum_tensor(name, [P, 512], F32))

        def sem(name):
            return ctx.enter_context(nc.semaphore(name))

        ident = sb("ident", [P, P])
        minus_half = sb("minus_half", [P, GB])
        b1_col = sb("b1_col", [P, C])
        b2_col = sb("b2_col", [P, C])
        b3_all = sb("b3_all", [P, GB, F])
        raw = {k: sb(f"{k}_raw", [P, C, F]) for k in ("w1", "w2", "w3", "wv")}
        qk_raw = sb("qk_raw", [P, C, 2 * F])
        qT = sb("qT", [P, C, F])
        kT = sb("kT", [P, C, F])
        hi = {k: sb(f"{k}_hi", [P, C, F], F32R) for k in ("w1", "w2", "w3", "wv", "m")}
        lo = {k: sb(f"{k}_lo", [P, C, F], F32R) for k in ("w1", "w2", "w3", "wv", "m")}

        x_in = ring("x_in", RING, [P, GB, F])
        adj_in = ring("adj_in", RING, [P, GB, P])
        mask_col = ring("mask_col", RING, [P, GB])
        mask_row = ring("mask_row", RING, [GB, P])
        x_b3 = ring("x_b3", RING, [P, GB, F])
        stats1 = ring("stats1", 2, [P, GB, 6])
        stats2 = ring("stats2", 2, [P, GB, 6])
        mv1 = ring("mv1", 2, [P, GB, 2])
        mv2 = ring("mv2", 2, [P, GB, 2])
        neg_mean1 = ring("neg_mean1", 2, [P, GB])
        neg_mean2 = ring("neg_mean2", 2, [P, GB])
        shift1 = ring("shift1", 2, [P, GB])
        shift2 = ring("shift2", 2, [P, GB])
        ve1 = ring("ve1", 2, [P, GB])
        ve2 = ring("ve2", 2, [P, GB])
        rstd1 = ring("rstd1", 2, [P, GB])
        rstd2 = ring("rstd2", 2, [P, GB])
        h_full = ring("h_full", 2, [P, GB, F])
        h_hi = ring("h_hi", 2, [P, GB, F], F32R)
        h_lo = ring("h_lo", 2, [P, GB, F], F32R)
        aT = ring("aT", RING, [P, GB, 2, P], F32R)
        aT_hi = [t[:, :, 0, :] for t in aT]
        aT_lo = [t[:, :, 1, :] for t in aT]
        zT_part = ring("zT_part", 2, [P, C, GB, P])
        zT_full = ring("zT_full", 2, [P, C, GB, P])
        zT_hi = ring("zT_hi", 2, [P, C, GB, P], F32R)
        zT_lo = ring("zT_lo", 2, [P, C, GB, P], F32R)
        o1_full = ring("o1_full", 2, [P, C, GB, P])
        o1_hi = ring("o1_hi", 2, [P, C, GB, P], F32R)
        o1_lo = ring("o1_lo", 2, [P, C, GB, P], F32R)
        s2_hi = ring("s2_hi", 2, [P, GB, F], F32R)
        s2_lo = ring("s2_lo", 2, [P, GB, F], F32R)
        o2_part = ring("o2_part", 2, [P, C, GB, P])
        o2_full = ring("o2_full", 2, [P, C, GB, P])
        o2_hi = ring("o2_hi", 2, [P, C, GB, P], F32R)
        o2_lo = ring("o2_lo", 2, [P, C, GB, P], F32R)
        s3_hi = ring("s3_hi", 2, [P, GB, F], F32R)
        s3_lo = ring("s3_lo", 2, [P, GB, F], F32R)
        x1 = ring("x1", RING, [P, GB, F])
        h2_full = ring("h2_full", 2, [P, GB, F])
        h2m_hi = ring("h2m_hi", 2, [P, GB, F], F32R)
        h2m_lo = ring("h2m_lo", 2, [P, GB, F], F32R)
        agg = ring("agg", 2, [P, GB, F])
        h2T_hi = ring("h2T_hi", 2, [P, C, GB, P], F32R)
        h2T_lo = ring("h2T_lo", 2, [P, C, GB, P], F32R)
        weighed = ring("weighed", GB, [P, F])
        w_col = ring("w_col", 2, [P, GB])
        w_row = ring("w_row", 2, [GB, P])
        w_max = ring("w_max", 2, [GB, 1])
        w_negmax = ring("w_negmax", 2, [GB, 1])
        e_row = ring("e_row", 2, [GB, P])
        e_sum = ring("e_sum", 2, [GB, 1])
        e_inv = ring("e_inv", 2, [GB, 1])
        p_row = ring("p_row", 2, [GB, P])
        p_col = ring("p_col", 2, [P, GB])

        banks = ctx.enter_context(nc.psum_tensor("banks", [P, 8, 512], F32))

        def chunk_first(b):
            return banks[:, b, :].rearrange("p (c g n) -> p c g n", c=C, g=GB)

        def graph_first(b):
            return banks[:, b, :].rearrange("p (g f) -> p g f", g=GB)

        def two_parts(b):
            return banks[:, b:b + C, :].rearrange("p c (g t n) -> p c g t n", g=GB, t=2)

        ps_zT, ps_o2 = two_parts(1), two_parts(1)
        ps_aT = banks[:, 3, 0:GB * P].rearrange("p (g n) -> p g n", g=GB)
        ps_o1, ps_h2T = chunk_first(6), chunk_first(5)
        ps_s2, ps_s3, ps_x1 = graph_first(0), graph_first(3), graph_first(4)
        ps_t, ps_agg, ps_v = graph_first(7), graph_first(6), graph_first(4)
        ps_wrow, ps_pcol = banks[0:GB, 5, 0:P], banks[:, 1, P:P + GB]
        ps_qT, ps_kT, ps_m = graph_first(4), graph_first(0), graph_first(7)

        weight_loaded = {k: sem(f"{k}_loaded") for k in ("w1", "w2", "w3", "wv", "qk")}
        bias_loaded = sem("bias_loaded")
        ident_zeroed = sem("ident_zeroed")
        const_made = sem("const_made")
        waits_passed = sem("waits_passed")
        weight_hi_made = {k: sem(f"{k}_hi_made") for k in ("w1", "w2", "w3", "wv", "m")}
        weight_lo_made = {k: sem(f"{k}_lo_made") for k in ("w1", "w2", "w3", "wv", "m")}
        q_turned = sem("q_turned")
        k_turned = sem("k_turned")
        qT_copied = sem("qT_copied")
        kT_copied = sem("kT_copied")
        m_multiplied = sem("m_multiplied")
        x_loaded = [sem(f"x_loaded{k}") for k in range(RING)]
        adj_loaded = [sem(f"adj_loaded{k}") for k in range(RING)]
        mask_loaded = [sem(f"mask_loaded{k}") for k in range(RING)]
        row_loaded = [sem(f"row_loaded{k}") for k in range(RING)]
        out_stored = [sem(f"out_stored{k}") for k in range(RING)]
        x_b3_made = sem("x_b3_made")
        stats1_made = sem("stats1_made")
        stats2_made = sem("stats2_made")
        mv1_made = sem("mv1_made")
        mv2_made = sem("mv2_made")
        ve1_made = sem("ve1_made")
        ve2_made = sem("ve2_made")
        rstd1_made = sem("rstd1_made")
        rstd2_made = sem("rstd2_made")
        shift1_made = sem("shift1_made")
        shift2_made = sem("shift2_made")
        h_full_made = sem("h_full_made")
        h_hi_made = sem("h_hi_made")
        h_lo_made = sem("h_lo_made")
        aT_done = sem("aT_done")
        aT_hi_made = sem("aT_hi_made")
        aT_lo_made = sem("aT_lo_made")
        zT_done = sem("zT_done")
        zT_part_made = sem("zT_part_made")
        zT_full_made = sem("zT_full_made")
        zT_hi_made = sem("zT_hi_made")
        zT_lo_made = sem("zT_lo_made")
        o1_done = sem("o1_done")
        o1_full_made = sem("o1_full_made")
        o1_hi_made = sem("o1_hi_made")
        o1_lo_made = sem("o1_lo_made")
        s2_done = sem("s2_done")
        s2_hi_made = sem("s2_hi_made")
        s2_lo_made = sem("s2_lo_made")
        o2_done = sem("o2_done")
        o2_part_made = sem("o2_part_made")
        o2_full_made = sem("o2_full_made")
        o2_hi_made = sem("o2_hi_made")
        o2_lo_made = sem("o2_lo_made")
        s3_done = sem("s3_done")
        s3_hi_made = sem("s3_hi_made")
        s3_lo_made = sem("s3_lo_made")
        x1_done = sem("x1_done")
        x1_made = sem("x1_made")
        h2T_done = sem("h2T_done")
        h2T_hi_made = sem("h2T_hi_made")
        h2T_lo_made = sem("h2T_lo_made")
        w_col_made = sem("w_col_made")
        w_turned = sem("w_turned")
        w_row_made = sem("w_row_made")
        w_negmax_made = sem("w_negmax_made")
        e_made = sem("e_made")
        e_inv_made = sem("e_inv_made")
        p_row_made = sem("p_row_made")
        p_turned = sem("p_turned")
        p_col_made = sem("p_col_made")
        v_done = sem("v_done")
        h2_full_made = sem("h2_full_made")
        h2m_hi_made = sem("h2m_hi_made")
        h2m_lo_made = sem("h2m_lo_made")
        agg_done = sem("agg_done")
        agg_made = sem("agg_made")
        t_done = sem("t_done")
        out_made = sem("out_made")

        def standing_wait(eng, made, count):
            eng.wait_ge(made, count)
            eng.sem_inc(waits_passed, 1)

        def free(eng, read, p):
            if p.exists(PAIRS):
                eng.wait_ge(read, p.done())

        def first(p):
            return isinstance(p.i, int) and p.c == 0

        def rounds(eng, one_round):
            for u in range(FIRST):
                one_round(lambda n: Pair(0, u - n))
            with eng.Fori(0, LOOPS, 1) as i:
                for j in range(RING):
                    one_round(lambda n: Pair(i, FIRST + j - n))
            for u in range(TAIL, ROUNDS):
                one_round(lambda n: Pair(0, u - n))

        block = ctx.enter_context(nc.Block())

        @block.sync
        def _(sp):
            def load_x(p):
                k, old = p.c % RING, p.back(RING)
                if old.exists(PAIRS):
                    sp.wait_ge(h_full_made, old.done())
                    sp.wait_ge(x_b3_made, old.done())
                rows = x[bass.ds(p.number() * GB, GB)]
                sp.dma_start(x_in[k][:], rows.rearrange("g n f -> n g f")).then_inc(x_loaded[k], 16)

            def load_adj(p):
                k, old = p.c % RING, p.back(RING)
                if old.exists(PAIRS):
                    sp.wait_ge(aT_done, old.done())
                rows = adj[bass.ds(p.number() * GB, GB)]
                sp.dma_start(adj_in[k][:], rows.rearrange("g n m -> n g m")).then_inc(adj_loaded[k], 16)

            def load(p):
                if p.exists(PAIRS):
                    load_x(p)
                    load_adj(p)

            def load_mask(p):
                if p.exists(PAIRS):
                    k, old = p.c % RING, p.back(RING)
                    rows = mask[bass.ds(p.number() * GB, GB)]
                    if old.exists(PAIRS):
                        sp.wait_ge(h2m_lo_made, old.done())
                        sp.wait_ge(w_row_made, old.done())
                    with nc.allow_non_contiguous_dma(reason="two short mask columns"):
                        sp.dma_start(mask_col[k][:], rows.rearrange("g n -> n g")).then_inc(mask_loaded[k], 16)
                    sp.dma_start(mask_row[k][:], rows).then_inc(row_loaded[k], 16)

            def store(p):
                if p.exists(PAIRS):
                    k = p.c % RING
                    sp.wait_ge(out_made, p.done())
                    sp.dma_start(out[bass.ds(p.number() * GB, GB)].rearrange("g n f -> n g f"), x1[k][:]).then_inc(out_stored[k], 16)

            def load_weight(name, dst, src):
                sp.dma_start(dst[:], src.rearrange("(c f) h -> f c h", f=P)).then_inc(weight_loaded[name], 16)

            load_x(Pair(0, 0))
            load_weight("qk", qk_raw, Wqk)
            load_adj(Pair(0, 0))
            load_weight("w1", raw["w1"], W1)
            load(Pair(0, 1))
            load_weight("w2", raw["w2"], W2)
            load_weight("w3", raw["w3"], W3)
            load_weight("wv", raw["wv"], Wv)

            def one_round(at):
                load_mask(at(2))
                store(at(5))
                load(at(-AHEAD))

            rounds(sp, one_round)
            for k in range(RING):
                sp.wait_ge(out_stored[k], 16 * (PAIRS // RING))

        @block.gpsimd
        def _(pool):
            pool.memset(ident[:], 0.0).then_inc(ident_zeroed, 1)
            pool.memset(minus_half[:], -0.5).then_inc(const_made, 1)
            pool.wait_ge(ident_zeroed, 1)
            pool.affine_select(out=ident[:], in_=ident[:], compare_op=ALU.not_equal, fill=1.0, base=0,
                               pattern=[[-1, P]], channel_multiplier=1).then_inc(const_made, 1)
            pool.wait_ge(const_made, 2)

            def minus_mean_and_ve(p, mv_made, mv, neg_mean, ve, ve_made):
                k = p.c % 2
                standing_wait(pool, mv_made, p.done())
                pool.tensor_scalar(ve[k][:], mv[k][:, :, 1], EPS, None, ALU.add).then_inc(ve_made, 1)
                pool.tensor_scalar(neg_mean[k][:], mv[k][:, :, 0], -1.0, None, ALU.mult).then_inc(ve_made, 1)

            def power(p, ve_made, ve, rstd, rstd_made):
                k = p.c % 2
                pool.wait_ge(ve_made, p.done() + p.done())
                pool.tensor_tensor(rstd[k][:], ve[k][:], minus_half[:], ALU.pow).then_inc(rstd_made, 1)

            def times_mean(p, rstd_made, rstd, neg_mean, shift, shift_made):
                k = p.c % 2
                pool.wait_ge(rstd_made, p.done())
                pool.tensor_tensor(shift[k][:], neg_mean[k][:], rstd[k][:], ALU.mult).then_inc(shift_made, 1)

            def w3_low(p):
                if not first(p):
                    return
                pool.wait_ge(weight_hi_made["w3"], 1)
                pool.tensor_tensor(lo["w3"][:], raw["w3"][:], hi["w3"][:].bitcast(F32), ALU.subtract).then_inc(weight_lo_made["w3"], 1)

            def variance2(p):
                if not p.exists(PAIRS):
                    return
                minus_mean_and_ve(p, mv2_made, mv2, neg_mean2, ve2, ve2_made)

            def power2(p):
                if not p.exists(PAIRS):
                    return
                power(p, ve2_made, ve2, rstd2, rstd2_made)

            def minus_mean_rstd2(p):
                if not p.exists(PAIRS):
                    return
                times_mean(p, rstd2_made, rstd2, neg_mean2, shift2, shift2_made)

            def add_b3(p):
                if not p.exists(PAIRS):
                    return
                r = p.c % RING
                pool.wait_ge(x_loaded[r], p.landed())
                if first(p):
                    pool.wait_ge(bias_loaded, 64)
                pool.tensor_tensor(x_b3[r][:], x_in[r][:], b3_all[:], ALU.add).then_inc(x_b3_made, 1)

            def o1_low(p):
                if not p.exists(PAIRS):
                    return
                k = p.c % 2
                pool.wait_ge(o1_hi_made, p.done())
                pool.tensor_tensor(o1_lo[k][:], o1_full[k][:], o1_hi[k][:].bitcast(F32), ALU.subtract).then_inc(o1_lo_made, 1)

            def wv_low(p):
                if not first(p):
                    return
                pool.wait_ge(weight_hi_made["wv"], 1)
                pool.tensor_tensor(lo["wv"][:], raw["wv"][:], hi["wv"][:].bitcast(F32), ALU.subtract).then_inc(weight_lo_made["wv"], 1)

            def variance1(p):
                if not p.exists(PAIRS):
                    return
                minus_mean_and_ve(p, mv1_made, mv1, neg_mean1, ve1, ve1_made)

            def power1(p):
                if not p.exists(PAIRS):
                    return
                power(p, ve1_made, ve1, rstd1, rstd1_made)

            def minus_mean_rstd1(p):
                if not p.exists(PAIRS):
                    return
                times_mean(p, rstd1_made, rstd1, neg_mean1, shift1, shift1_made)

            def zT_low(p):
                if not p.exists(PAIRS):
                    return
                k = p.c % 2
                pool.wait_ge(zT_hi_made, p.done())
                pool.tensor_tensor(zT_lo[k][:], zT_full[k][:], zT_hi[k][:].bitcast(F32), ALU.subtract).then_inc(zT_lo_made, 1)

            def one_round(at):
                w3_low(at(3))
                variance2(at(4))
                power2(at(4))
                minus_mean_rstd2(at(4))
                add_b3(at(1))
                o1_low(at(2))
                wv_low(at(3))
                variance1(at(0))
                power1(at(0))
                minus_mean_rstd1(at(0))
                zT_low(at(1))

            rounds(pool, one_round)

        @block.scalar
        def _(act):
            with nc.allow_non_contiguous_dma(reason="two short bias columns"):
                act.dma_start(b1_col[:], b1.rearrange("(c h) -> h c", h=P)).then_inc(bias_loaded, 16)
                act.dma_start(b2_col[:], b2.rearrange("(c h) -> h c", h=P)).then_inc(bias_loaded, 16)
            for g in range(GB):
                act.dma_start(b3_all[:, g, :], b3.partition_broadcast(P)).then_inc(bias_loaded, 16)

            def high_of_weight(p, name):
                if first(p):
                    act.wait_ge(weight_loaded[name], 16)
                    nc.scalar.activation(hi[name][:], raw[name][:], ACT.Copy).then_inc(weight_hi_made[name], 1)

            def scaled(p, src, rstd, shift, shift_made, dst, made):
                k = p.c % 2
                act.wait_ge(shift_made, p.done())
                for g in range(GB):
                    last = nc.scalar.activation(dst[k][:, g], src[p.c % RING][:, g], ACT.Relu, bias=shift[k][:, g:g + 1],
                                                scale=rstd[k][:, g:g + 1])
                last.then_inc(made, 1)

            def zT_high(p):
                if not p.exists(PAIRS):
                    return
                k = p.c % 2
                act.wait_ge(zT_full_made, p.done())
                nc.scalar.activation(zT_hi[k][:], zT_full[k][:], ACT.Copy).then_inc(zT_hi_made, 1)

            def w3_high(p):
                if not first(p):
                    return
                high_of_weight(p, "w3")

            def aT_high(p):
                if not p.exists(PAIRS):
                    return
                r = p.c % RING
                free(act, agg_done, p.back(4))
                act.wait_ge(aT_done, p.done())
                nc.scalar.activation(aT_hi[r], ps_aT, ACT.Copy).then_inc(aT_hi_made, 1)

            def copy_agg(p):
                if not p.exists(PAIRS):
                    return
                k = p.c % 2
                act.wait_ge(agg_done, p.done())
                nc.scalar.activation(agg[k][:], ps_agg, ACT.Copy).then_inc(agg_made, 1)

            def exp_w(p):
                if not p.exists(PAIRS):
                    return
                k = p.c % 2
                act.wait_ge(w_negmax_made, p.done())
                nc.scalar.activation(e_row[k][:], w_row[k][:], ACT.Exp, bias=w_negmax[k][:, 0:1],
                                     accum_out=e_sum[k][:, 0:1]).then_inc(e_made, 1)

            def o2_lows_part(p):
                if not p.exists(PAIRS):
                    return
                k = p.c % 2
                act.wait_ge(o2_done, p.done())
                for c in range(C):
                    last = nc.scalar.activation(o2_part[k][:, c], ps_o2[:, c, :, 1], ACT.Identity, bias=b2_col[:, c:c + 1])
                last.then_inc(o2_part_made, 1)

            def h_whole(p):
                if not p.exists(PAIRS):
                    return
                scaled(p, x_in, rstd1, shift1, shift1_made, h_full, h_full_made)

            def softmax_row(p):
                if not p.exists(PAIRS):
                    return
                k = p.c % 2
                act.wait_ge(e_inv_made, p.done())
                nc.scalar.activation(p_row[k][:], e_row[k][:], ACT.Copy, scale=e_inv[k][:, 0:1]).then_inc(p_row_made, 1)

            def wv_high(p):
                if not first(p):
                    return
                high_of_weight(p, "wv")

            def o2_high(p):
                if not p.exists(PAIRS):
                    return
                k = p.c % 2
                act.wait_ge(o2_full_made, p.done())
                nc.scalar.activation(o2_hi[k][:], o2_full[k][:], ACT.Relu).then_inc(o2_hi_made, 1)

            def w1_high(p):
                if not first(p):
                    return
                high_of_weight(p, "w1")

            def o1_whole(p):
                if not p.exists(PAIRS):
                    return
                k = p.c % 2
                if first(p):
                    act.wait_ge(bias_loaded, 64)
                act.wait_ge(o1_done, p.done())
                for c in range(C):
                    last = nc.scalar.activation(o1_full[k][:, c], ps_o1[:, c], ACT.Relu, bias=b1_col[:, c:c + 1])
                last.then_inc(o1_full_made, 1)

            def softmax_col(p):
                if not p.exists(PAIRS):
                    return
                k = p.c % 2
                act.wait_ge(p_turned, p.done())
                nc.scalar.activation(p_col[k][:], ps_pcol, ACT.Copy).then_inc(p_col_made, 1)

            def h2_whole(p):
                if not p.exists(PAIRS):
                    return
                scaled(p, x1, rstd2, shift2, shift2_made, h2_full, h2_full_made)

            def negative_max(p):
                if not p.exists(PAIRS):
                    return
                k = p.c % 2
                act.wait_ge(w_row_made, p.done())
                nc.scalar.activation(w_negmax[k][:], w_max[k][:], ACT.Copy, scale=-1.0).then_inc(w_negmax_made, 1)

            def copy_qT(p):
                if not first(p):
                    return
                act.wait_ge(q_turned, 1)
                nc.scalar.activation(qT[:], ps_qT, ACT.Copy).then_inc(qT_copied, 1)

            def m_high(p):
                if not first(p):
                    return
                act.wait_ge(m_multiplied, 1)
                nc.scalar.activation(hi["m"][:], ps_m, ACT.Copy).then_inc(weight_hi_made["m"], 1)

            def s3_high(p):
                if not p.exists(PAIRS):
                    return
                k = p.c % 2
                act.wait_ge(s3_done, p.done())
                nc.scalar.activation(s3_hi[k][:], ps_s3, ACT.Copy).then_inc(s3_hi_made, 1)

            def h2m_high(p):
                if not p.exists(PAIRS):
                    return
                k, r = p.c % 2, p.c % RING
                act.wait_ge(mask_loaded[r], p.landed())
                act.wait_ge(h2_full_made, p.done())
                for g in range(GB):
                    last = nc.scalar.activation(h2m_hi[k][:, g], h2_full[k][:, g], ACT.Copy, scale=mask_col[r][:, g:g + 1])
                last.then_inc(h2m_hi_made, 1)

            def zT_lows_part(p):
                if not p.exists(PAIRS):
                    return
                k = p.c % 2
                act.wait_ge(zT_done, p.done())
                nc.scalar.activation(zT_part[k][:], ps_zT[:, :, :, 1], ACT.Copy).then_inc(zT_part_made, 1)

            def w2_high(p):
                if not first(p):
                    return
                high_of_weight(p, "w2")

            def s2_high(p):
                if not p.exists(PAIRS):
                    return
                k = p.c % 2
                act.wait_ge(s2_done, p.done())
                nc.scalar.activation(s2_hi[k][:], ps_s2, ACT.Copy).then_inc(s2_hi_made, 1)

            def h2T_high(p):
                if not p.exists(PAIRS):
                    return
                k = p.c % 2
                act.wait_ge(h2T_done, p.done())
                nc.scalar.activation(h2T_hi[k][:], ps_h2T, ACT.Copy).then_inc(h2T_hi_made, 1)

            def one_round(at):
                zT_high(at(1))
                w3_high(at(2))
                aT_high(at(0))
                copy_agg(at(4))
                exp_w(at(5))
                o2_lows_part(at(2))
                h_whole(at(0))
                softmax_row(at(5))
                wv_high(at(1))
                o2_high(at(2))
                w1_high(at(0))
                o1_whole(at(1))
                softmax_col(at(5))
                h2_whole(at(3))
                negative_max(at(4))
                copy_qT(at(0))
                m_high(at(1))
                s3_high(at(2))
                h2m_high(at(3))
                zT_lows_part(at(0))
                w2_high(at(0))
                s2_high(at(1))
                h2T_high(at(3))

            rounds(act, one_round)

        @block.vector
        def _(dve):
            def statistics(p, src, stats, stats_made):
                for g in range(GB):
                    last = nc.vector.bn_stats(stats[p.c % 2][:, g, :], src[:, g, :])
                last.then_inc(stats_made, 1)

            def mean_and_variance(p, stats_made, stats, mv, mv_made):
                k = p.c % 2
                standing_wait(dve, stats_made, p.done())
                for g in range(GB):
                    last = nc.vector.bn_aggr(mv[k][:, g, :], stats[k][:, g, :])
                last.then_inc(mv_made, 1)

            def add_parts(p, part_made, ps, part, full, made):
                k = p.c % 2
                dve.wait_ge(part_made, p.done())
                nc.vector.tensor_tensor(full[k][:], ps[:, :, :, 0], part[k][:], ALU.add).then_inc(made, 1)

            def statistics1(p):
                if not p.exists(PAIRS):
                    return
                r = p.c % RING
                dve.wait_ge(x_loaded[r], p.landed())
                statistics(p, x_in[r], stats1, stats1_made)

            def copy_kT(p):
                if not first(p):
                    return
                dve.wait_ge(k_turned, 1)
                nc.vector.tensor_copy(kT[:], ps_kT).then_inc(kT_copied, 1)

            def s3_low(p):
                if not p.exists(PAIRS):
                    return
                k = p.c % 2
                dve.wait_ge(s3_hi_made, p.done())
                nc.vector.tensor_tensor(s3_lo[k][:], ps_s3, s3_hi[k][:].bitcast(F32), ALU.subtract).then_inc(s3_lo_made, 1)

            def mean_variance1(p):
                if not p.exists(PAIRS):
                    return
                mean_and_variance(p, stats1_made, stats1, mv1, mv1_made)

            def h2m_low(p):
                if not p.exists(PAIRS):
                    return
                k, r = p.c % 2, p.c % RING
                dve.wait_ge(h2m_hi_made, p.done())
                for g in range(GB):
                    last = nc.vector.scalar_tensor_tensor(out=h2m_lo[k][:, g], in0=h2_full[k][:, g], scalar=mask_col[r][:, g:g + 1],
                                                          in1=h2m_hi[k][:, g].bitcast(F32), op0=ALU.mult, op1=ALU.subtract)
                last.then_inc(h2m_lo_made, 1)

            def zT_whole(p):
                if not p.exists(PAIRS):
                    return
                add_parts(p, zT_part_made, ps_zT, zT_part, zT_full, zT_full_made)

            def m_low(p):
                if not first(p):
                    return
                dve.wait_ge(weight_hi_made["m"], 1)
                nc.vector.tensor_tensor(lo["m"][:], ps_m, hi["m"][:].bitcast(F32), ALU.subtract).then_inc(weight_lo_made["m"], 1)

            def s2_low(p):
                if not p.exists(PAIRS):
                    return
                k = p.c % 2
                dve.wait_ge(s2_hi_made, p.done())
                nc.vector.tensor_tensor(s2_lo[k][:], ps_s2, s2_hi[k][:].bitcast(F32), ALU.subtract).then_inc(s2_lo_made, 1)

            def residual(p):
                if not p.exists(PAIRS):
                    return
                r = p.c % RING
                dve.wait_ge(x1_done, p.done())
                dve.wait_ge(x_b3_made, p.done())
                if p.back(RING).exists(PAIRS):
                    dve.wait_ge(out_stored[r], p.back(RING).landed())
                nc.vector.tensor_tensor(x1[r][:], ps_x1, x_b3[r][:], ALU.add).then_inc(x1_made, 1)

            def h2T_low(p):
                if not p.exists(PAIRS):
                    return
                k = p.c % 2
                dve.wait_ge(h2T_hi_made, p.done())
                nc.vector.tensor_tensor(h2T_lo[k][:], ps_h2T, h2T_hi[k][:].bitcast(F32), ALU.subtract).then_inc(h2T_lo_made, 1)

            def statistics2(p):
                if not p.exists(PAIRS):
                    return
                r = p.c % RING
                dve.wait_ge(x1_made, p.done())
                statistics(p, x1[r], stats2, stats2_made)

            def w1_low(p):
                if not first(p):
                    return
                dve.wait_ge(weight_hi_made["w1"], 1)
                nc.vector.tensor_tensor(lo["w1"][:], raw["w1"][:], hi["w1"][:].bitcast(F32), ALU.subtract).then_inc(weight_lo_made["w1"], 1)

            def aT_low(p):
                if not p.exists(PAIRS):
                    return
                r = p.c % RING
                dve.wait_ge(aT_hi_made, p.done())
                nc.vector.tensor_tensor(aT_lo[r], ps_aT, aT_hi[r].bitcast(F32), ALU.subtract).then_inc(aT_lo_made, 1)

            def inverse_sum(p):
                if not p.exists(PAIRS):
                    return
                k = p.c % 2
                dve.wait_ge(e_made, p.done())
                nc.vector.reciprocal(e_inv[k][:], e_sum[k][:]).then_inc(e_inv_made, 1)

            def mean_variance2(p):
                if not p.exists(PAIRS):
                    return
                mean_and_variance(p, stats2_made, stats2, mv2, mv2_made)

            def w2_low(p):
                if not first(p):
                    return
                dve.wait_ge(weight_hi_made["w2"], 1)
                nc.vector.tensor_tensor(lo["w2"][:], raw["w2"][:], hi["w2"][:].bitcast(F32), ALU.subtract).then_inc(weight_lo_made["w2"], 1)

            def o2_whole(p):
                if not p.exists(PAIRS):
                    return
                add_parts(p, o2_part_made, ps_o2, o2_part, o2_full, o2_full_made)

            def weights(p):
                if not p.exists(PAIRS):
                    return
                k = p.c % 2
                dve.wait_ge(t_done, p.done())
                dve.wait_ge(agg_made, p.done())
                for g in range(GB):
                    last = nc.vector.tensor_tensor_reduce(
                        out=weighed[g][:], in0=ps_t[:, g], in1=agg[k][:, g], scale=1.0, scalar=0.0, op0=ALU.mult, op1=ALU.add,
                        accum_out=w_col[k][:, g:g + 1])
                last.then_inc(w_col_made, 1)

            def h_high(p):
                if not p.exists(PAIRS):
                    return
                k = p.c % 2
                dve.wait_ge(h_full_made, p.done())
                nc.vector.tensor_copy(h_hi[k][:], h_full[k][:]).then_inc(h_hi_made, 1)

            def o2_low(p):
                if not p.exists(PAIRS):
                    return
                k = p.c % 2
                dve.wait_ge(o2_hi_made, p.done())
                nc.vector.scalar_tensor_tensor(out=o2_lo[k][:], in0=o2_full[k][:], scalar=0.0, in1=o2_hi[k][:].bitcast(F32),
                                               op0=ALU.max, op1=ALU.subtract).then_inc(o2_lo_made, 1)

            def h_low(p):
                if not p.exists(PAIRS):
                    return
                k = p.c % 2
                dve.wait_ge(h_hi_made, p.done())
                nc.vector.tensor_tensor(h_lo[k][:], h_full[k][:], h_hi[k][:].bitcast(F32), ALU.subtract).then_inc(h_lo_made, 1)

            def o1_high(p):
                if not p.exists(PAIRS):
                    return
                k = p.c % 2
                dve.wait_ge(o1_full_made, p.done())
                nc.vector.tensor_copy(o1_hi[k][:], o1_full[k][:]).then_inc(o1_hi_made, 1)

            def mask_weights(p):
                if not p.exists(PAIRS):
                    return
                k, r = p.c % 2, p.c % RING
                dve.wait_ge(w_turned, p.done())
                standing_wait(dve, row_loaded[r], p.landed())
                nc.vector.tensor_tensor_reduce(out=w_row[k][:], in0=ps_wrow, in1=mask_row[r][:], scale=SCALE, scalar=-3.4e38,
                                               op0=ALU.mult, op1=ALU.max, accum_out=w_max[k][:, 0:1]).then_inc(w_row_made, 1)

            def output(p):
                if not p.exists(PAIRS):
                    return
                k, r = p.c % 2, p.c % RING
                dve.wait_ge(v_done, p.done())
                dve.wait_ge(p_col_made, p.done())
                for g in range(GB):
                    last = nc.vector.scalar_tensor_tensor(out=x1[r][:, g], in0=ps_v[:, g], scalar=p_col[k][:, g:g + 1],
                                                          in1=x1[r][:, g], op0=ALU.mult, op1=ALU.add)
                last.then_inc(out_made, 1)

            def one_round(at):
                statistics1(at(0))
                copy_kT(at(1))
                s3_low(at(3))
                mean_variance1(at(0))
                h2m_low(at(4))
                zT_whole(at(1))
                m_low(at(3))
                s2_low(at(2))
                residual(at(3))
                h2T_low(at(4))
                statistics2(at(3))
                w1_low(at(1))
                aT_low(at(0))
                inverse_sum(at(5))
                mean_variance2(at(3))
                w2_low(at(1))
                o2_whole(at(2))
                weights(at(4))
                h_high(at(0))
                o2_low(at(2))
                h_low(at(0))
                o1_high(at(1))
                mask_weights(at(4))
                output(at(5))

            rounds(dve, one_round)

        @block.tensor
        def _(pe):
            pe.wait_ge(const_made, 2)

            def weight_ready(p, name):
                if first(p):
                    pe.wait_ge(weight_lo_made[name], 1)

            def turn_weight(ps, offset, done):
                for d in range(C):
                    for f in range(C):
                        last = nc.tensor.transpose(ps[:, d, f * P:(f + 1) * P],
                                                   qk_raw[:, f, offset + d * P:offset + (d + 1) * P], ident[:])
                last.then_inc(done, 1)

            def bank_free(p, last_user, *others):
                users = (last_user,) + (others if isinstance(p.i, int) else ())
                for read, n in users:
                    free(pe, read, p.back(n))

            def bank_free_of_weight(p, n, read):
                if isinstance(p.i, int) and p.c == n:
                    pe.wait_ge(read, 1)

            def halves(terms, last_pass, lo_made, p, done):
                def emit(passes, first, final):
                    n = 0
                    for o, left_hi, left_lo, right_hi, right_lo in terms:
                        for which in passes:
                            left = left_lo if which == "left" else left_hi
                            right = right_lo if which == "right" else right_hi
                            n += 1
                            last = nc.tensor.matmul(o, left, right, start=first and n == 1,
                                                    stop=final and n == len(terms) * len(passes), skip_group_check=True)
                    return last

                emit(("high", "left" if last_pass == "right" else "right"), True, False)
                pe.wait_ge(lo_made, p.done())
                emit((last_pass,), False, True).then_inc(done, 1)

            def cut(t, c):
                return t[:, c * P:(c + 1) * P]

            def with_adj(ps, left_hi, left_lo, r, lo_made, p, done):
                for c in range(C):
                    for g in range(GB):
                        nc.tensor.matmul(ps[:, c, g], cut(left_hi[:, g], c), aT[r][:, g], start=g == 0, stop=False,
                                         skip_group_check=True)
                pe.wait_ge(lo_made, p.done())
                for c in range(C):
                    for g in range(GB):
                        last = nc.tensor.matmul(ps[:, c, g, 0], cut(left_lo[:, g], c), aT_hi[r][:, g], start=False,
                                                stop=g == GB - 1, skip_group_check=True)
                last.then_inc(done, 1)

            graphs_chunks = [(g, c) for g in range(GB) for c in range(C)]

            def product_s3(p):
                if not p.exists(PAIRS):
                    return
                k = p.c % 2
                weight_ready(p, "w3")
                pe.wait_ge(o2_hi_made, p.done())
                bank_free(p, (aT_lo_made, -2), (s3_lo_made, 1))
                halves([(ps_s3[:, g], o2_hi[k][:, c, g], o2_lo[k][:, c, g], hi["w3"][:, c], lo["w3"][:, c])
                        for g, c in graphs_chunks], "left", o2_lo_made, p, s3_done)

            def product_zT(p):
                if not p.exists(PAIRS):
                    return
                k, r = p.c % 2, p.c % RING
                pe.wait_ge(h_hi_made, p.done())
                pe.wait_ge(aT_lo_made, p.done())
                bank_free(p, (p_col_made, 5), (o2_full_made, 2), (zT_full_made, 1))
                bank_free(p, (o2_full_made, 2), (zT_full_made, 1))
                with_adj(ps_zT, h_hi[k], h_lo[k], r, h_lo_made, p, zT_done)

            def product_s2(p):
                if not p.exists(PAIRS):
                    return
                k = p.c % 2
                weight_ready(p, "w2")
                pe.wait_ge(o1_hi_made, p.done())
                bank_free(p, (s2_lo_made, 1))
                bank_free_of_weight(p, 0, kT_copied)
                halves([(ps_s2[:, g], o1_hi[k][:, c, g], o1_lo[k][:, c, g], hi["w2"][:, c], lo["w2"][:, c])
                        for g, c in graphs_chunks], "left", o1_lo_made, p, s2_done)

            def transpose_h2(p):
                if not p.exists(PAIRS):
                    return
                k = p.c % 2
                pe.wait_ge(h2_full_made, p.done())
                bank_free(p, (w_row_made, 1), (h2T_lo_made, 1))
                for g, c in graphs_chunks:
                    last = nc.tensor.transpose(ps_h2T[:, c, g], cut(h2_full[k][:, g], c), ident[:])
                last.then_inc(h2T_done, 1)

            def product_x1(p):
                if not p.exists(PAIRS):
                    return
                k, r = p.c % 2, p.c % RING
                pe.wait_ge(s3_hi_made, p.done())
                bank_free(p, (out_made, 3), (x1_made, 1))
                bank_free_of_weight(p, 0, qT_copied)
                halves([(ps_x1[:, g], aT_hi[r][:, g], aT_lo[r][:, g], s3_hi[k][:, g], s3_lo[k][:, g]) for g in range(GB)],
                       "right", s3_lo_made, p, x1_done)

            def transpose_adj(p):
                if not p.exists(PAIRS):
                    return
                r = p.c % RING
                pe.wait_ge(adj_loaded[r], p.landed())
                bank_free(p, (s3_lo_made, 3), (aT_lo_made, 1))
                for g in range(GB):
                    last = nc.tensor.transpose(ps_aT[:, g], adj_in[r][:, g], ident[:])
                last.then_inc(aT_done, 1)

            def turn_wq(p):
                if not first(p):
                    return
                pe.wait_ge(weight_loaded["qk"], 16)
                bank_free(p, (x1_made, 3), (out_made, 6))
                turn_weight(ps_qT, 0, q_turned)

            def product_agg(p):
                if not p.exists(PAIRS):
                    return
                k, r = p.c % 2, p.c % RING
                pe.wait_ge(h2m_hi_made, p.done())
                bank_free(p, (o1_full_made, -2), (agg_made, 1))
                halves([(ps_agg[:, g], aT_hi[r][:, g], aT_lo[r][:, g], h2m_hi[k][:, g], h2m_lo[k][:, g]) for g in range(GB)],
                       "right", h2m_lo_made, p, agg_done)

            def product_o2(p):
                if not p.exists(PAIRS):
                    return
                k, r = p.c % 2, p.c % RING
                pe.wait_ge(s2_hi_made, p.done())
                bank_free(p, (zT_full_made, -1), (p_col_made, 4), (o2_full_made, 1))
                bank_free(p, (zT_full_made, -1), (o2_full_made, 1))
                with_adj(ps_o2, s2_hi[k], s2_lo[k], r, s2_lo_made, p, o2_done)

            def product_t(p):
                if not p.exists(PAIRS):
                    return
                k = p.c % 2
                weight_ready(p, "m")
                pe.wait_ge(h2T_hi_made, p.done())
                bank_free(p, (w_col_made, 1))
                bank_free_of_weight(p, 0, weight_lo_made["m"])
                halves([(ps_t[:, g], h2T_hi[k][:, c, g], h2T_lo[k][:, c, g], hi["m"][:, c], lo["m"][:, c])
                        for g, c in graphs_chunks], "left", h2T_lo_made, p, t_done)

            def turn_wk(p):
                if not first(p):
                    return
                pe.wait_ge(weight_loaded["qk"], 16)
                bank_free(p, (s2_lo_made, 2))
                turn_weight(ps_kT, F, k_turned)

            def multiply_m(p):
                if not first(p):
                    return
                pe.wait_ge(qT_copied, 1)
                pe.wait_ge(kT_copied, 1)
                bank_free(p, (w_col_made, 3))
                for f in range(C):
                    for d in range(C):
                        last = nc.tensor.matmul(ps_m[:, f, :], qT[:, d, f * P:(f + 1) * P], kT[:, d, :],
                                                start=d == 0, stop=d == C - 1)
                last.then_inc(m_multiplied, 1)

            def product_o1(p):
                if not p.exists(PAIRS):
                    return
                k = p.c % 2
                weight_ready(p, "w1")
                pe.wait_ge(zT_hi_made, p.done())
                bank_free(p, (agg_made, 3), (o1_full_made, 1))
                halves([(ps_o1[:, h], cut(hi["w1"][:, c], h), cut(lo["w1"][:, c], h), zT_hi[k][:, c], zT_lo[k][:, c])
                        for h in range(C) for c in range(C)], "right", zT_lo_made, p, o1_done)

            def product_v(p):
                if not p.exists(PAIRS):
                    return
                k = p.c % 2
                weight_ready(p, "wv")
                bank_free(p, (x1_made, -2), (out_made, 1))
                bank_free_of_weight(p, 0, qT_copied)
                halves([(ps_v[:, g], h2T_hi[k][:, c, g], h2T_lo[k][:, c, g], hi["wv"][:, c], lo["wv"][:, c])
                        for g, c in graphs_chunks], "left", h2T_lo_made, p, v_done)

            def turn_p(p):
                if not p.exists(PAIRS):
                    return
                k = p.c % 2
                bank_free(p, (o2_full_made, -3), (zT_full_made, -4), (p_col_made, 1))
                standing_wait(pe, p_row_made, p.done())
                nc.tensor.transpose(ps_pcol, p_row[k][:], ident[0:GB, 0:GB]).then_inc(p_turned, 1)

            def turn_w(p):
                if not p.exists(PAIRS):
                    return
                k = p.c % 2
                pe.wait_ge(w_col_made, p.done())
                bank_free(p, (h2T_lo_made, 0), (w_row_made, 1))
                nc.tensor.transpose(ps_wrow, w_col[k][:], ident[:]).then_inc(w_turned, 1)

            def one_round(at):
                product_s3(at(3))
                product_zT(at(1))
                product_s2(at(2))
                transpose_h2(at(4))
                product_x1(at(3))
                transpose_adj(at(0))
                turn_wq(at(0))
                product_agg(at(4))
                product_o2(at(2))
                product_t(at(4))
                turn_wk(at(0))
                multiply_m(at(1))
                product_o1(at(1))
                product_v(at(5))
                turn_p(at(5))
                turn_w(at(4))

            rounds(pe, one_round)


_INS = ["x", "adj", "nodemask", "L0_gnn_W1", "L0_gnn_b1", "L0_gnn_W2", "L0_gnn_b2", "L0_gnn_W3", "L0_gnn_b3",
        "L1_gnn_Wqk", "L1_gnn_Wv"]


def kernel(**inputs):
    import numpy as np
    import concourse.bacc as bacc
    from concourse.bass_utils import run_bass_kernel_spmd

    nc = bacc.Bacc("TRN2", target_bir_lowering=False, num_devices=1)
    arrays, args = {}, []
    for name in _INS:
        a = np.ascontiguousarray(inputs[name])
        arrays[f"in_{name}"] = a
        args.append(nc.dram_tensor(f"in_{name}", a.shape, mybir.dt.from_np(a.dtype), kind="ExternalInput").ap())
    result = nc.dram_tensor("out_0", arrays["in_x"].shape, F32, kind="ExternalOutput").ap()
    gnn_kernel(nc, *args, result)
    r = run_bass_kernel_spmd(nc, [arrays], core_ids=[0])
    return r.results[0]["out_0"]
```
